# Optimizing a Trainium2 kernel written in Bass

```python
import numpy as np
import jax
import jax.numpy as jnp

def _softmax(x, axis=-1):
    return jax.nn.softmax(x, axis=axis)

def _gelu(x):
    return jax.nn.gelu(x, approximate=True)

def _silu(x):
    return jax.nn.silu(x)

def _sigmoid(x):
    return jax.nn.sigmoid(x)

def _layernorm(x, axis=-1, eps=1e-05):
    m = jnp.mean(x, axis=axis, keepdims=True)
    v = jnp.var(x, axis=axis, keepdims=True)
    return (x - m) / jnp.sqrt(v + eps)

def _scatter_add(tgt, idx, src, axis=0):
    return tgt.at[idx].add(src)

def _segment_sum(src, seg, n):
    return jax.ops.segment_sum(src, seg, n)
kernel_name = 'mk_lm_tower_d1_tok_ids768_r4_8e33c2'

def setup_inputs(seed: int=0):
    np.random.seed(seed)
    _w = jnp.asarray

    def _rec_inputs():
        import jax
        import jax.numpy as jnp
        _rk = jax.random.key(seed)
        x = jax.random.randint(jax.random.fold_in(_rk, 1), (64, 256), 0, 12564, jnp.int32)
        return x
    x = _rec_inputs()

    def _L0_tok_setup():
        import jax, jax.numpy as jnp
        import numpy as np
        QMAX = 127.0
        key = jax.random.key(seed)
        k1, k2, k3 = jax.random.split(key, 3)
        vocab, d = (50257, 192)
        B, S = (8, 512)
        x = jax.random.randint(k1, (B, S), 0, vocab, dtype=jnp.int64)
        weight = jax.random.normal(k2, (vocab, d), dtype=jnp.float32)
        weight_scale = jax.random.uniform(k3, (1,), dtype=jnp.float32, minval=0.01, maxval=1.0)
        return {'x': x, 'weight': weight, 'weight_scale': weight_scale}
    _L0_tok_all = _L0_tok_setup()
    _L0_tok_in = {k: v for k, v in _L0_tok_all.items() if k in ('weight', 'weight_scale')}
    del _L0_tok_all

    def _L0_attn_setup():
        import jax, jax.numpy as jnp
        import numpy as np
        NUM_HEADS = 12

        def _l2_dist(Q):
            sq = jnp.sum(Q * Q, axis=-1)
            d2 = sq[..., :, None] + sq[..., None, :] - 2.0 * jnp.einsum('bhnd,bhmd->bhnm', Q, Q)
            d2 = jnp.maximum(d2, 0.0)
            return jnp.where(d2 > 0, jnp.sqrt(jnp.where(d2 > 0, d2, 1.0)), 0.0)
        key = jax.random.key(seed)
        k1, k2, k3 = jax.random.split(key, 3)
        B, N, E = (8, 256, 192)
        x = jax.random.normal(k1, (B, N, E), dtype=jnp.float32)
        W_qkv = jax.random.normal(k2, (2 * E, E), dtype=jnp.float32) * E ** (-0.5)
        W_out = jax.random.normal(k3, (E, E), dtype=jnp.float32) * E ** (-0.5)
        b_out = jnp.zeros((E,), dtype=jnp.float32)
        return {'x': x, 'W_qkv': W_qkv, 'W_out': W_out, 'b_out': b_out}
    _L0_attn_all = _L0_attn_setup()
    _L0_attn_in = {k: v for k, v in _L0_attn_all.items() if k in ('W_qkv', 'W_out', 'b_out')}
    del _L0_attn_all

    def _L0_ffn_setup():
        import math
        import jax, jax.numpy as jnp
        import numpy as np
        B, L, D = (8, 1024, 192)
        E = 16
        TOP_K = 2
        F_EXP = 4 * D
        F_SH = F_EXP * 2 // 4
        key = jax.random.key(seed)
        ks = jax.random.split(key, 8)
        s = lambda fan_in: 1.0 / math.sqrt(fan_in)
        return {'hidden_states': jax.random.normal(ks[0], (B, L, D), jnp.float32), 'gate_weight': jax.random.uniform(ks[1], (E, D), jnp.float32, -s(D), s(D)), 'Wg': jax.random.uniform(ks[2], (E, F_EXP, D), jnp.float32, -s(D), s(D)), 'Wu': jax.random.uniform(ks[3], (E, F_EXP, D), jnp.float32, -s(D), s(D)), 'Wd': jax.random.uniform(ks[4], (E, D, F_EXP), jnp.float32, -s(F_EXP), s(F_EXP)), 'Ws_g': jax.random.uniform(ks[5], (F_SH, D), jnp.float32, -s(D), s(D)), 'Ws_u': jax.random.uniform(ks[6], (F_SH, D), jnp.float32, -s(D), s(D)), 'Ws_d': jax.random.uniform(ks[7], (D, F_SH), jnp.float32, -s(F_SH), s(F_SH))}
    _L0_ffn_all = _L0_ffn_setup()
    _L0_ffn_in = {k: v for k, v in _L0_ffn_all.items() if k in ('gate_weight', 'Wg', 'Wu', 'Wd', 'Ws_g', 'Ws_u', 'Ws_d')}
    del _L0_ffn_all
    return {'x': x, 'L0_tok_weight': _L0_tok_in['weight'], 'L0_tok_weight_scale': _L0_tok_in['weight_scale'], 'L0_attn_W_qkv': _L0_attn_in['W_qkv'], 'L0_attn_W_out': _L0_attn_in['W_out'], 'L0_attn_b_out': _L0_attn_in['b_out'], 'L0_ffn_gate_weight': _L0_ffn_in['gate_weight'], 'L0_ffn_Wg': _L0_ffn_in['Wg'], 'L0_ffn_Wu': _L0_ffn_in['Wu'], 'L0_ffn_Wd': _L0_ffn_in['Wd'], 'L0_ffn_Ws_g': _L0_ffn_in['Ws_g'], 'L0_ffn_Ws_u': _L0_ffn_in['Ws_u'], 'L0_ffn_Ws_d': _L0_ffn_in['Ws_d']}

def reference(x, L0_tok_weight, L0_tok_weight_scale, L0_attn_W_qkv, L0_attn_W_out, L0_attn_b_out, L0_ffn_gate_weight, L0_ffn_Wg, L0_ffn_Wu, L0_ffn_Wd, L0_ffn_Ws_g, L0_ffn_Ws_u, L0_ffn_Ws_d):
    import jax
    import jax.numpy as jnp

    def _L0_tok_ref(x, weight, weight_scale):
        import jax, jax.numpy as jnp
        import numpy as np
        QMAX = 127.0
        w = jnp.round(jnp.clip(weight / weight_scale, -QMAX, QMAX))
        out = jnp.take(w, x, axis=0) * weight_scale
        return out.astype(jnp.float32)

    def _L0_attn_ref(x, W_qkv, W_out, b_out):
        import jax, jax.numpy as jnp
        import numpy as np
        NUM_HEADS = 12

        def _l2_dist(Q):
            sq = jnp.sum(Q * Q, axis=-1)
            d2 = sq[..., :, None] + sq[..., None, :] - 2.0 * jnp.einsum('bhnd,bhmd->bhnm', Q, Q)
            d2 = jnp.maximum(d2, 0.0)
            return jnp.where(d2 > 0, jnp.sqrt(jnp.where(d2 > 0, d2, 1.0)), 0.0)
        B, N, E = x.shape
        H = NUM_HEADS
        D = E // H
        scale = D ** (-0.5)
        qkv = x @ W_qkv.T
        qk, v = jnp.split(qkv, 2, axis=-1)
        Q = qk.reshape(B, N, H, D).transpose(0, 2, 1, 3)
        V = v.reshape(B, N, H, D).transpose(0, 2, 1, 3)
        dist = _l2_dist(Q)
        attn = jax.nn.softmax(-dist * scale, axis=-1)
        out = jnp.einsum('bhnm,bhmd->bhnd', attn, V)
        out = out.transpose(0, 2, 1, 3).reshape(B, N, E)
        return out @ W_out.T + b_out

    def _L0_ffn_ref(hidden_states, gate_weight, Wg, Wu, Wd, Ws_g, Ws_u, Ws_d):
        import math
        import jax, jax.numpy as jnp
        import numpy as np
        B, L, D = (8, 1024, 192)
        E = 16
        TOP_K = 2
        F_EXP = 4 * D
        F_SH = F_EXP * 2 // 4
        b, l, d = hidden_states.shape
        n = b * l
        x = hidden_states.reshape(n, d)
        scores = jax.nn.sigmoid(x @ gate_weight.T)
        capacity = math.ceil(n / E * TOP_K)
        topk_score, topk_ids = jax.lax.top_k(scores.T, capacity)
        xg = x[topk_ids]
        gate = jax.nn.silu(jnp.einsum('ecd,efd->ecf', xg, Wg))
        up = jnp.einsum('ecd,efd->ecf', xg, Wu)
        out = jnp.einsum('ecf,edf->ecd', gate * up, Wd)
        out = out * topk_score[..., None]
        y = jnp.zeros((n, d), x.dtype).at[topk_ids.reshape(-1)].add(out.reshape(-1, d))
        y = y.reshape(b, l, d)
        shared = jax.nn.silu(hidden_states @ Ws_g.T) * (hidden_states @ Ws_u.T) @ Ws_d.T
        return y + shared
    h = _L0_tok_ref(x, L0_tok_weight, L0_tok_weight_scale)
    h = h + _L0_attn_ref(_layernorm(h, axis=-1), L0_attn_W_qkv, L0_attn_W_out, L0_attn_b_out)
    h = h + _L0_ffn_ref(_layernorm(h, axis=-1), L0_ffn_gate_weight, L0_ffn_Wg, L0_ffn_Wu, L0_ffn_Wd, L0_ffn_Ws_g, L0_ffn_Ws_u, L0_ffn_Ws_d)
    return h

_drawn_inputs = setup_inputs


def setup_inputs(seed=0):
    import zlib

    import numpy as np

    out = dict(_drawn_inputs(seed))
    spreads = {'L0_attn_b_out': (0.0, 0.1)}
    factors = {}
    for name, (base, spread) in spreads.items():
        noise = np.random.default_rng([zlib.crc32(name.encode()), seed]).standard_normal(out[name].shape)
        drawn = base * np.exp(spread * noise) if base else spread * noise
        out[name] = jnp.asarray(drawn.astype(out[name].dtype))
    for name, factor in factors.items():
        out[name] = (out[name] * factor).astype(out[name].dtype)
    return out
```

```python
from contextlib import ExitStack

import numpy as np

import concourse.bass as bass
from concourse import mybir

ALU = mybir.AluOpType
ACT = mybir.ActivationFunctionType
AX = mybir.AxisListType
F32 = mybir.dt.float32
F16 = mybir.dt.float16
I32 = mybir.dt.int32
U32 = mybir.dt.uint32

P = 128
D = 192
REST = D - P
HEADS = 12
HD = D // HEADS
SEQ = 256
STEPS = SEQ // P
PACK = 3 * P
SPLIT = 64.0
CHUNKS = ((0, 0), (1, 1), (2, 0), (3, 1), (0, 2))
EPS = 1e-5
QMAX = 127.0
ROUND = 1.5 * 2.0 ** 23
VROW = HEADS * (HD + 1)
GROUP = 4


class At:

    def __init__(self, turn, period, c):
        self.turn, self.period, self.c = turn, period, c

    def back(self, lag):
        return At(self.turn, self.period, self.c - lag)

    def times(self, k, plus=0):
        return self.turn * (self.period * k) + (self.c * k + plus)

    def slot(self, m):
        return self.c % m

    def use(self, m, k=1, plus=0):
        return self.turn * (self.period // m * k) + (self.c // m * k + plus)

    def live(self, n):
        return not isinstance(self.turn, int) or 0 <= self.c < n


def run_steps(eng, n, lead, lag, period, step):
    low = -(-(lag + 3) // period) * period
    high = max((n - lead) // period * period, 0)
    if high - low < 2 * period:
        low = high = n
    for i in range(-lead, low):
        step(At(0, period, i))
    if high > low:
        with eng.Fori(low // period, high // period) as turn:
            for c in range(period):
                step(At(turn, period, c))
    for i in range(high, n + lag):
        step(At(0, period, i))


def need(eng, sem, value, apart=None):
    if not isinstance(value, int) or value > 0:
        eng.wait_ge(sem, value)
        if apart is not None and not isinstance(value, int):
            eng.sem_inc(apart, 1)


class Mem:

    def __init__(self, nc, name):
        self.nc, self.name, self.ctx = nc, name, ExitStack()
        self.used = []

    def __enter__(self):
        self.ctx.__enter__()
        return self

    def __exit__(self, *e):
        done = self.ctx.__exit__(*e)
        if self.used:
            self.nc.clear_and_free_semaphores(self.used)
            self.nc.all_engine_barrier()
        return done

    def sb(self, name, shape, dt):
        return self.ctx.enter_context(self.nc.sbuf_tensor(f"{self.name}_{name}", shape, dt))

    def ps(self, name, shape, dt):
        return self.ctx.enter_context(self.nc.psum_tensor(f"{self.name}_{name}", shape, dt))

    def bank(self, name, dt=F32):
        return self.ps(name, [P, 2048 // (4 if dt == F32 else 2)], dt)

    def sem(self, name):
        self.used.append(self.nc.alloc_semaphore(name=f"{self.name}_{name}"))
        return self.used[-1]

    def sems(self, name, n):
        return [self.sem(f"{name}{i}") for i in range(n)]

    def block(self):
        return self.ctx.enter_context(self.nc.Block())


def make_constants(nc, top, ws_dram, x_dram, dims):
    NT = dims["NT"]
    k = {
        "eye16": top.sb("eye16", [P, P], F16),
        "eye32": top.sb("eye32", [P, P], F32),
        "ws": top.sb("ws", [P, 1], F32),
        "inv_ws": top.sb("inv_ws", [P, 1], F32),
        "eps": top.sb("eps", [P, 1], F32),
        "ids": top.sb("ids", [P, NT], U32),
    }
    with Mem(nc, "const") as m:
        rows = m.sb("rows", [NT, P], I32)
        rowsf = m.sb("rowsf", [NT, P], F32)
        cols = m.bank("cols")[:, 0:NT]
        loaded, zeroed, made = m.sem("loaded"), m.sem("zeroed"), m.sem("made")
        floats, turned, done = m.sem("floats"), m.sem("turned"), m.sem("done")
        block = m.block()

        @block.sync
        def _(sp):
            sp.dma_start(rows[:], x_dram).then_inc(loaded, 16)
            sp.dma_start(k["ws"][:], ws_dram.to_broadcast([P, 1])).then_inc(loaded, 16)

        @block.gpsimd
        def _(pool):
            nc.gpsimd.memset(k["eye16"][:], 0.0).then_inc(zeroed, 1)
            nc.gpsimd.memset(k["eye32"][:], 0.0).then_inc(zeroed, 1)
            pool.wait_ge(zeroed, 2)
            for eye in (k["eye16"], k["eye32"]):
                nc.gpsimd.affine_select(out=eye[:], in_=eye[:], compare_op=ALU.not_equal, fill=1.0, base=0,
                                        pattern=[[-1, P]], channel_multiplier=1).then_inc(made, 1)

        @block.vector
        def _(dve):
            nc.vector.memset(k["eps"][:], EPS)
            dve.wait_ge(loaded, 32)
            nc.vector.tensor_copy(rowsf[:], rows[:]).then_inc(floats, 1)
            nc.vector.reciprocal(k["inv_ws"][:], k["ws"][:])
            dve.wait_ge(turned, 1)
            nc.vector.tensor_copy(k["ids"][:], cols).then_inc(done, 1)

        @block.tensor
        def _(pe):
            pe.wait_ge(made, 2)
            pe.wait_ge(floats, 1)
            pe.transpose(cols, rowsf[:], k["eye32"][0:NT, 0:NT]).then_inc(turned, 1)
    return k


def make_stacks(nc, k, name, jobs):
    tiles = jobs
    with Mem(nc, name) as m:
        nat = m.sb("nat", [P, 2, D], F32)
        parts = m.sb("parts", [P, 2, 4 * P], F16)
        turned = [m.bank(f"turned{i}", F16)[:, 0:4 * P].rearrange("p (c n) -> p c n", c=4) for i in range(2)]
        loaded = m.sems("loaded", 2)
        hi_done, lo_done, twice, turned_done, kept = (m.sem(x) for x in ("hi", "lo", "twice", "turned_done", "kept"))
        block = m.block()

        @block.sync
        def _(sp):
            for i, (src, n, dst) in enumerate(tiles):
                need(sp, lo_done, i - 1)
                sp.dma_start(nat[0:n, i % 2, :], src).then_inc(loaded[i % 2], 16)

        @block.scalar
        def _(act):
            for i, (src, n, dst) in enumerate(tiles):
                act.wait_ge(loaded[i % 2], 16 * (i // 2 + 1))
                need(act, turned_done, i - 1)
                nc.scalar.activation(parts[0:n, i % 2, 0:D], nat[0:n, i % 2, :], ACT.Copy,
                                     scale=SPLIT).then_inc(hi_done, 1)

        @block.vector
        def _(dve):
            for i, (src, n, dst) in enumerate(tiles):
                dve.wait_ge(hi_done, i + 1)
                nc.vector.scalar_tensor_tensor(out=parts[0:n, i % 2, 2 * P:2 * P + D], in0=nat[0:n, i % 2, :],
                                               scalar=SPLIT, in1=parts[0:n, i % 2, 0:D], op0=ALU.mult,
                                               op1=ALU.subtract).then_inc(lo_done, 1)
                dve.wait_ge(turned_done, i + 1)
                block_of = turned[i % 2][:, :, 0:n]
                if len(dst.shape) == 4:
                    block_of = block_of.rearrange("p c (a b) -> p c a b", b=dst.shape[3])
                nc.vector.tensor_copy(dst, block_of).then_inc(kept, 1)

        @block.gpsimd
        def _(pool):
            for i, (src, n, dst) in enumerate(tiles):
                pool.wait_ge(lo_done, i + 1)
                for c in (0, 2 * P):
                    last = nc.gpsimd.tensor_copy(parts[0:n, i % 2, c + D:c + 2 * P], parts[0:n, i % 2, c + P:c + D])
                last.then_inc(twice, 1)

        @block.tensor
        def _(pe):
            for i, (src, n, dst) in enumerate(tiles):
                pe.wait_ge(twice, i + 1)
                need(pe, kept, i - 1)
                for c in range(4):
                    last = pe.transpose(turned[i % 2][:, c, 0:n], parts[0:n, i % 2, c * P:(c + 1) * P],
                                        k["eye16"][0:n, 0:n])
                last.then_inc(turned_done, 1)


def row_jobs(src, n, stack):
    return [(src[r:min(r + P, n), :], min(P, n - r), stack[:, :, r:min(r + P, n)]) for r in range(0, n, P)]


def query_jobs(src, stack):
    by_head = stack.rearrange("p c (d h) -> p c h d", h=HEADS)
    heads = P // HD
    return [(src[r:min(r + P, D), :], min(P, D - r), by_head[:, :, r // HD:min(r // HD + heads, HEADS), :])
            for r in range(0, D, P)]


def embed_and_project(nc, k, dims, emb, b_out, wqkv, stack_dram, v_dram, h_dram):
    NB = dims["NB"]
    with Mem(nc, "emb") as m:
        picked = m.sb("picked", [P, 2, STEPS], U32)
        picked_done, apart = m.sem("picked_done"), m.sem("apart")
        row = m.sb("row", [P, 2, STEPS, D], F32)
        q = m.sb("q", [P, 2, STEPS, D], F32)
        h0 = m.sb("h0", [P, 2, STEPS, D], F32)
        hb = m.sb("hb", [P, 2, STEPS, D], F32)
        stats = m.sb("stats", [P, 2, STEPS, 6], F32)
        mv = m.sb("mv", [P, 2, STEPS, 2], F32)
        std = m.sb("std", [P, 2, STEPS], F32)
        rstd = m.sb("rstd", [P, 2, STEPS], F32)
        xn = m.sb("xn", [P, 2, STEPS, D], F32)
        pack = m.sb("pack", [P, 2, STEPS, PACK], F16)
        chunks = m.sb("chunks", [P, 2, 3, SEQ], F16)
        bias = m.sb("bias", [P, D], F32)
        wide_picks = m.sb("wide_picks", [P, 2, HEADS, HD], F32)
        picks = m.sb("picks", [P, 2, HEADS], F32)
        q_parts = m.sb("q_parts", [P, 2, 2, 2, SEQ], F16)
        q_sq = m.sb("q_sq", [P, 2, SEQ], F32)
        s_parts = m.sb("s_parts", [HEADS, 2, 2, SEQ], F16)
        vals = m.sb("vals", [P, 2, STEPS, VROW], F32)
        chunk_bank = m.bank("chunk_ps", F16)
        chunk_ps = chunk_bank[:].rearrange("p (c n) -> p c n", n=SEQ)
        q_ps = [m.bank(f"q_ps{i}")[:].rearrange("p (c n) -> p c n", n=SEQ) for i in range(2)]
        v_ps = [m.bank(f"v_ps{i}")[:, 0:STEPS * D].rearrange("p (s d) -> p s d", d=D) for i in range(2)]
        s_ps = [m.bank(f"s_ps{i}")[0:HEADS, 0:SEQ] for i in range(2)]
        (bias_in, quarters, set_up, h0_done, scaled, clipped, rounded, hb_done, stat_done, aggr_done, std_done, rstd_done,
         xn_done, hi_done, lo_done, turned, chunks_done, q_mm, v_mm, qhi_done, qlo_done, qsq_done, v_done,
         s_mm, shi_done, slo_done) = (m.sem(x) for x in (
             "bias_in", "quarters", "set_up", "h0_done", "scaled", "clipped", "rounded", "hb_done", "stat_done", "aggr_done",
             "std_done", "rstd_done", "xn_done", "hi_done", "lo_done", "turned", "chunks_done", "q_mm",
             "v_mm", "qhi_done", "qlo_done", "qsq_done", "v_done", "s_mm", "shi_done", "slo_done"))
        got = m.sems("got", 2)
        h_out, v_out, stack_out = m.sems("h_out", 2), m.sems("v_out", 2), m.sems("stack_out", 2)
        inv = 1.0 / SPLIT
        WRITES = 3
        block = m.block()

        @block.gpsimd
        def _(pool):
            nc.gpsimd.memset(wide_picks[:], 0.0).then_inc(quarters, 1)
            pool.wait_ge(quarters, 1)
            for half in range(2):
                nc.gpsimd.affine_select(out=wide_picks[:, half], in_=wide_picks[:, half], compare_op=ALU.not_equal,
                                        fill=-0.5, base=P * half, pattern=[[-1, HEADS], [-HEADS, HD]],
                                        channel_multiplier=1).then_inc(quarters, 1)

            def step(i):
                t = i.back(-1)
                if t.live(NB):
                    a = t.slot(2)
                    need(pool, scaled, t.times(1, -1))
                    nc.gpsimd.tensor_copy(picked[:, a, :], ids_of(t)).then_inc(picked_done, 1)
                    need(pool, picked_done, t.times(1, 1), apart)
                    for s in range(STEPS):
                        nc.gpsimd.indirect_dma_start(
                            out=row[:, a, s, :], out_offset=None, in_=emb,
                            in_offset=bass.IndirectOffsetOnAxis(ap=picked[:, a, s:s + 1], axis=0)).then_inc(got[a], 16)
                t = i.back(1)
                if t.live(NB):
                    pool.wait_ge(hi_done, t.times(1, 1))
                    a = t.slot(2)
                    nc.gpsimd.tensor_tensor(pack[:, a, :, D:2 * P], xn[:, a, :, P:D], pack[:, a, :, P:D], ALU.subtract)
                    nc.gpsimd.tensor_tensor(pack[:, a, :, 2 * P:PACK], xn[:, a, :, 0:P], pack[:, a, :, 0:P],
                                            ALU.subtract).then_inc(lo_done, 1)

            def ids_of(t):
                if isinstance(t.turn, int):
                    return k["ids"][:, STEPS * t.c:STEPS * t.c + STEPS]
                return k["ids"][:, bass.ds(t.times(STEPS), STEPS)]

            run_steps(pool, NB, 1, 1, 2, step)

        @block.vector
        def _(dve):
            for a in range(2):
                nc.vector.memset(vals[:, a], 1.0)
            nc.vector.memset(chunk_bank[:].bitcast(F32), 0.0).then_inc(set_up, 1)
            dve.wait_ge(quarters, 3)
            nc.vector.tensor_reduce(picks[:], wide_picks[:], AX.X, ALU.add).then_inc(set_up, 1)
            dve.wait_ge(bias_in, 16)

            def quantise(i):
                if not i.live(NB):
                    return
                a = i.slot(2)
                dve.wait_ge(got[a], i.use(2, 16 * STEPS, 16 * STEPS))
                nc.vector.tensor_scalar(q[:, a], row[:, a], k["inv_ws"][:], QMAX, ALU.mult, ALU.min).then_inc(scaled, 1)
                dve.wait_ge(scaled, i.times(1, 1))
                nc.vector.tensor_scalar(q[:, a], q[:, a], -QMAX, ROUND, ALU.max, ALU.add).then_inc(clipped, 1)
                need(dve, xn_done, i.times(1, -1))
                dve.wait_ge(clipped, i.times(1, 1))
                nc.vector.tensor_scalar(h0[:, a], q[:, a], -ROUND, k["ws"][:], ALU.add, ALU.mult).then_inc(h0_done, 1)
                dve.wait_ge(h0_done, i.times(1, 1))
                for s in range(STEPS):
                    last = nc.vector.bn_stats(stats[:, a, s, :], h0[:, a, s, :])
                last.then_inc(stat_done, 1)
                need(dve, h_out[a], i.use(2, 16))
                nc.vector.tensor_tensor(hb[:, a], h0[:, a], bias[:, None, :].to_broadcast([P, STEPS, D]),
                                        ALU.add).then_inc(hb_done, 1)
                need(dve, stat_done, i.times(1, 1), apart)
                for s in range(STEPS):
                    last = nc.vector.bn_aggr(mv[:, a, s, :], stats[:, a, s, :])
                last.then_inc(aggr_done, 1)

            def normalise(t):
                if not t.live(NB):
                    return
                a = t.slot(2)
                dve.wait_ge(std_done, t.times(1, 1))
                nc.vector.reciprocal(rstd[:, a], std[:, a]).then_inc(rstd_done, 1)
                dve.wait_ge(rstd_done, t.times(1, 1))
                need(dve, lo_done, t.times(1, -1))
                for s in range(STEPS):
                    last = nc.vector.tensor_scalar(xn[:, a, s, :], h0[:, a, s, :], mv[:, a, s, 0:1], rstd[:, a, s:s + 1],
                                                   ALU.subtract, ALU.mult)
                last.then_inc(xn_done, 1)

            def query_rest(t):
                if not t.live(NB):
                    return
                a = t.slot(2)
                dve.wait_ge(qhi_done, t.times(1, 1))
                need(dve, stack_out[a], t.use(2, 16 * WRITES))
                for half, n in ((0, P), (1, REST)):
                    last = nc.vector.scalar_tensor_tensor(
                        out=q_parts[0:n, a, 1, half, :], in0=q_ps[a][0:n, half, :], scalar=inv,
                        in1=q_parts[0:n, a, 0, half, :], op0=ALU.mult, op1=ALU.subtract)
                last.then_inc(qlo_done, 1)

            def square_rest(t):
                if t.live(NB):
                    dve.wait_ge(shi_done, t.times(1, 1))
                    nc.vector.tensor_tensor(s_parts[:, t.slot(2), 1, :], s_ps[t.slot(2)], s_parts[:, t.slot(2), 0, :],
                                            ALU.subtract).then_inc(slo_done, 1)

            def step(i):
                normalise(i.back(1))
                quantise(i)
                query_rest(i.back(4))
                square_rest(i.back(4))

            run_steps(dve, NB, 0, 4, 2, step)

        @block.scalar
        def _(act):
            act.wait_ge(set_up, 1)

            def deviations(t):
                if t.live(NB):
                    a = t.slot(2)
                    act.wait_ge(aggr_done, t.times(1, 1))
                    need(act, rstd_done, t.times(1, -1))
                    nc.scalar.activation(std[:, a], mv[:, a, :, 1], ACT.Sqrt, bias=k["eps"][:]).then_inc(std_done, 1)

            def keep_queries(t):
                if t.live(NB):
                    a = t.slot(2)
                    act.wait_ge(q_mm, t.times(1, 1))
                    need(act, s_mm, t.times(1, 0))
                    nc.scalar.activation(q_sq[:, 0, :], q_ps[a][:, 0, :], ACT.Square, scale=inv)
                    nc.scalar.activation(q_sq[0:REST, 1, :], q_ps[a][0:REST, 1, :], ACT.Square,
                                         scale=inv).then_inc(qsq_done, 1)
                    need(act, stack_out[a], t.use(2, 16 * WRITES))
                    for half, n in ((0, P), (1, REST)):
                        last = nc.scalar.activation(q_parts[0:n, a, 0, half, :], q_ps[a][0:n, half, :], ACT.Copy, scale=inv)
                    last.then_inc(qhi_done, 1)

            def keep_values(t):
                if t.live(NB):
                    a = t.slot(2)
                    act.wait_ge(v_mm, t.times(1, 1))
                    need(act, v_out[a], t.use(2, 16))
                    nc.scalar.activation(
                        vals[:, a].rearrange("p s (h d) -> p (s h) d", d=HD + 1)[:, :, 0:HD],
                        v_ps[a].rearrange("p s (h d) -> p (s h) d", d=HD), ACT.Copy, scale=inv).then_inc(v_done, 1)

            def keep_chunks(t):
                if t.live(NB):
                    a = t.slot(2)
                    act.wait_ge(turned, t.times(1, 1))
                    need(act, v_mm, t.times(1, -1))
                    nc.scalar.copy(chunks[:, a], chunk_ps[:, 0:3]).then_inc(chunks_done, 1)

            def split(t):
                if t.live(NB):
                    a = t.slot(2)
                    act.wait_ge(xn_done, t.times(1, 1))
                    need(act, turned, t.times(1, -1))
                    nc.scalar.copy(pack[:, a, :, 0:D], xn[:, a]).then_inc(hi_done, 1)

            def keep_squares(t):
                if t.live(NB):
                    a = t.slot(2)
                    act.wait_ge(s_mm, t.times(1, 1))
                    nc.scalar.copy(s_parts[:, a, 0, :], s_ps[a]).then_inc(shi_done, 1)

            def step(i):
                deviations(i.back(1))
                keep_queries(i.back(4))
                keep_values(i.back(4))
                split(i.back(1))
                keep_chunks(i.back(2))
                keep_squares(i.back(4))

            run_steps(act, NB, 0, 4, 2, step)

        @block.tensor
        def _(pe):
            pe.wait_ge(set_up, 2)

            def step(i):
                t = i.back(3)
                if t.live(NB):
                    a = t.slot(2)
                    pe.wait_ge(chunks_done, t.times(1, 1))
                    need(pe, qlo_done, t.times(1, -1))
                    for half, n in ((0, P), (1, REST)):
                        for c, (w, x) in enumerate(CHUNKS):
                            last = pe.matmul(q_ps[a][0:n, half, :], wqkv[:, w, half * P:half * P + n], chunks[:, a, x, :],
                                             start=c == 0, stop=c == len(CHUNKS) - 1)
                    last.then_inc(q_mm, 1)
                    need(pe, v_done, t.times(1, -1))
                    for s in range(STEPS):
                        for c, (w, x) in enumerate(CHUNKS):
                            last = pe.matmul(v_ps[a][:, s, :], chunks[:, a, x, s * P:(s + 1) * P], wqkv[:, w, D:2 * D],
                                             start=c == 0, stop=c == len(CHUNKS) - 1)
                    last.then_inc(v_mm, 1)
                t = i.back(2)
                if t.live(NB):
                    a = t.slot(2)
                    pe.wait_ge(lo_done, t.times(1, 1))
                    need(pe, chunks_done, t.times(1, 0))
                    for s in range(STEPS):
                        for c in range(3):
                            last = pe.transpose(chunk_ps[:, c, s * P:(s + 1) * P], pack[:, a, s, c * P:(c + 1) * P], k["eye16"][:])
                    last.then_inc(turned, 1)
                t = i.back(4)
                if t.live(NB):
                    a = t.slot(2)
                    pe.wait_ge(qsq_done, t.times(1, 1))
                    need(pe, slo_done, t.times(1, -1))
                    pe.matmul(s_ps[a], picks[:, 0, :], q_sq[:, 0, :], start=True, stop=False)
                    pe.matmul(s_ps[a], picks[0:REST, 1, :], q_sq[0:REST, 1, :], start=False, stop=True).then_inc(s_mm, 1)

            run_steps(pe, NB, 0, 4, 2, step)

        @block.sync
        def _(sp):
            sp.dma_start(bias[:], b_out.to_broadcast([P, D])).then_inc(bias_in, 16)

            def step(i):
                t = i.back(4)
                if t.live(NB):
                    a = t.slot(2)
                    sp.wait_ge(v_done, t.times(1, 1))
                    sp.dma_start(v_dram[seq_of(t)], vals[:, a]).then_inc(v_out[a], 16)
                if i.live(NB):
                    sp.wait_ge(hb_done, i.times(1, 1))
                    sp.dma_start(h_dram[seq_of(i)], hb[:, i.slot(2)]).then_inc(h_out[i.slot(2)], 16)
                if t.live(NB):
                    sp.wait_ge(qlo_done, t.times(1, 1))
                    rows = stack_dram[seq_of(t)][0:2 * HD, :].rearrange("(c d) (h n) -> (d h) c n", c=2, h=HEADS)
                    for half, n in ((0, P), (1, REST)):
                        sp.dma_start(rows[half * P:half * P + n], q_parts[0:n, a, :, half, :]).then_inc(stack_out[a], 16)
                    sp.wait_ge(slo_done, t.times(1, 1))
                    sp.dma_start(stack_dram[seq_of(t)][2 * HD:2 * HD + 2, :].rearrange("c (h n) -> h c n", h=HEADS),
                                 s_parts[:, a]).then_inc(stack_out[a], 16)

            def seq_of(t):
                return t.c if isinstance(t.turn, int) else t.times(1)

            run_steps(sp, NB, 0, 4, 2, step)
            for a in range(2):
                uses = (NB - a + 1) // 2
                sp.wait_ge(h_out[a], 16 * uses)
                sp.wait_ge(v_out[a], 16 * uses)
                sp.wait_ge(stack_out[a], 16 * WRITES * uses)


def attention(nc, k, dims, w_out, mv, stack_dram, v_dram, h_dram, h1_dram):
    NB, group = dims["NB"], dims["group"]
    R = 2 * group
    lag, out, turned_at, post = R - 1, R, R + 1, R + 2
    inv = 1.0 / SPLIT
    W = 3 * P
    with Mem(nc, "att") as m:
        moving = m.sb("moving", [P, 2, HEADS, SEQ], F16)
        fixed = m.sb("fixed", [P, 2, HEADS, SEQ], F16)
        dist = [m.sb(f"dist{i}", [P, HEADS, W], F32) for i in range(R)]
        vals = m.sb("vals", [P, 2, STEPS * VROW + 2 * HD], F32)
        e10 = m.sb("e10", [P, 2, 4, P], F32)
        o_sb = m.sb("o_sb", [P, 3, SEQ], F32)
        recip = m.sb("recip", [P, STEPS, HEADS], F32)
        att = m.sb("att", [P, STEPS, D], F32)
        pack = m.sb("pack", [P, STEPS, PACK], F16)
        chunks = m.sb("chunks", [P, 3, SEQ], F16)
        hb = m.sb("hb", [P, 2, STEPS, D], F32)
        h1 = m.sb("h1", [P, 2, STEPS, D], F32)
        stats = m.sb("stats", [P, STEPS, 6], F32)
        d_ps = [m.bank(f"d_ps{i}") for i in range(3)]
        t_ps = m.bank("t_ps")[:].rearrange("p (h n) -> p h n", n=P)
        o_ps = m.ps("o_ps", [P, 4, SEQ], F32)
        x_ps = m.bank("x_ps")
        c_ps = m.bank("c_ps", F16)[:].rearrange("p (c n) -> p c n", n=SEQ)
        (set_up, dist_mm, clamped, rooted, exped, turned, e10_done, pv_done, o_done, ot_done, recip_done, att_done,
         hi_done, lo_done, xt_done, chunks_done, wo_done, h1_done, stat_done, aggr_done, apart) = (m.sem(x) for x in (
             "set_up", "dist_mm", "clamped", "rooted", "exped", "turned", "e10_done", "pv_done", "o_done", "ot_done",
             "recip_done", "att_done", "hi_done", "lo_done", "xt_done", "chunks_done", "wo_done", "h1_done",
             "stat_done", "aggr_done", "apart"))
        padded = m.sem("padded")
        stack_in, v_in, hb_in, h1_out = (m.sems(x, 2) for x in ("stack_in", "v_in", "hb_in", "h1_out"))
        LOADS = 8
        block = m.block()

        def at(dram, t):
            return dram[t.c if isinstance(t.turn, int) else t.times(1)]

        @block.gpsimd
        def _(pool):
            n = 0
            for rows, value in ((slice(64, P), 0.0), (slice(64, 68), 1.0)):
                for stack in (moving, fixed):
                    for a in range(2):
                        nc.gpsimd.memset(stack[rows, a], value).then_inc(set_up, 1)
                        n += 1
                        pool.wait_ge(set_up, n)

            def step(i):
                t = i.back(turned_at)
                if t.live(NB):
                    need(pool, att_done, t.times(2, 2), apart)
                    need(pool, xt_done, t.times(1, 0), apart)
                    nc.gpsimd.tensor_copy(pack[:, :, 0:D], att[:]).then_inc(hi_done, 1)
                    pool.wait_ge(hi_done, t.times(1, 1))
                    nc.gpsimd.tensor_tensor(pack[:, :, D:2 * P], att[:, :, P:D], pack[:, :, P:D], ALU.subtract)
                    nc.gpsimd.tensor_tensor(pack[:, :, 2 * P:PACK], att[:, :, 0:P], pack[:, :, 0:P],
                                            ALU.subtract).then_inc(lo_done, 1)

            run_steps(pool, NB, 0, post, R, step)

        @block.sync
        def _(sp):
            sp.wait_ge(set_up, 8)
            sp.wait_ge(padded, 1)

            def load(t):
                a = t.slot(2)
                need(sp, dist_mm, t.times(HEADS, -HEADS))
                rows = at(stack_dram, t)
                two = rows[0:2 * HD, :]
                def flat(x):
                    return x.rearrange("p h n -> p (h n)")
                sp.dma_start(flat(moving[0:2 * HD, a]), two).then_inc(stack_in[a], 16)
                sp.dma_start(flat(moving[2 * HD:4 * HD, a]), two).then_inc(stack_in[a], 16)
                sp.dma_start(flat(moving[64:66, a]), rows[2 * HD:2 * HD + 2, :]).then_inc(stack_in[a], 16)
                for part in range(2):
                    for copy in range(2):
                        at_row = (2 * part + copy) * HD
                        sp.dma_start(flat(fixed[at_row:at_row + HD, a]),
                                     rows[part * HD:(part + 1) * HD, :]).then_inc(stack_in[a], 16)
                sp.dma_start(flat(fixed[66:68, a]), rows[2 * HD:2 * HD + 2, :]).then_inc(stack_in[a], 16)

            def step(i):
                t = i.back(-1)
                if t.live(NB):
                    load(t)
                t = i.back(lag - 1)
                if t.live(NB):
                    a = t.slot(2)
                    need(sp, pv_done, t.times(3, -3))
                    sp.dma_start(vals[:, a, 0:STEPS * VROW].rearrange("p (s r) -> p s r", s=STEPS),
                                 at(v_dram, t)).then_inc(v_in[a], 16)
                t = i.back(post - 1)
                if t.live(NB):
                    a = t.slot(2)
                    need(sp, h1_done, t.times(1, -1))
                    sp.dma_start(hb[:, a], at(h_dram, t)).then_inc(hb_in[a], 16)
                t = i.back(post)
                if t.live(NB):
                    a = t.slot(2)
                    sp.wait_ge(h1_done, t.times(1, 1))
                    sp.dma_start(at(h1_dram, t), h1[:, a]).then_inc(h1_out[a], 16)

            run_steps(sp, NB, 1, post, R, step)
            for a in range(2):
                sp.wait_ge(h1_out[a], 16 * ((NB - a + 1) // 2))


        @block.tensor
        def _(pe):
            def distances(i, heads):
                if not i.live(NB):
                    return
                a = i.slot(2)
                for h in heads:
                    if h == 0:
                        pe.wait_ge(stack_in[a], i.use(2, 16 * LOADS, 16 * LOADS))
                    need(pe, clamped, i.times(HEADS, h - 2))
                    pe.matmul(d_ps[h % 3][:, 0:SEQ], fixed[:, a, h, 0:P], moving[:, a, h, :], start=True, stop=True)
                    pe.matmul(d_ps[h % 3][:, SEQ:W], fixed[:, a, h, P:SEQ], moving[:, a, h, P:SEQ],
                              start=True, stop=True).then_inc(dist_mm, 1)

            def turn(v, g):
                if v.live(NB):
                    pe.wait_ge(exped, v.times(3, g + 1))
                    need(pe, e10_done, v.times(3, g))
                    for h in range(4):
                        last = pe.transpose(t_ps[:, h, :], dist[v.slot(R)][:, 4 * g + h, P:SEQ], k["eye32"][:])
                    last.then_inc(turned, 1)

            def values(v, g):
                if not v.live(NB):
                    return
                a = v.slot(2)
                if g == 0:
                    pe.wait_ge(v_in[a], v.use(2, 16, 16))
                    need(pe, o_done, v.times(1, 0))
                e = dist[v.slot(R)]
                pe.wait_ge(e10_done, v.times(3, g + 1))
                for h in range(4):
                    q, col = slice(32 * h, 32 * h + 32), (4 * g + h) * (HD + 1)
                    pe.matmul(o_ps[q, g, :], vals[:, a, col:col + 32], e[:, 4 * g + h, 0:SEQ],
                              start=True, stop=False, skip_group_check=True)
                for h in range(4):
                    q, col = slice(32 * h, 32 * h + 32), VROW + (4 * g + h) * (HD + 1)
                    pe.matmul(o_ps[q, g, 0:P], vals[:, a, col:col + 32], e10[:, (v.slot(2) + g) % 2, h, :],
                              start=False, stop=True, skip_group_check=True)
                for h in range(4):
                    q, col = slice(32 * h, 32 * h + 32), VROW + (4 * g + h) * (HD + 1)
                    last = pe.matmul(o_ps[q, g, P:SEQ], vals[:, a, col:col + 32], e[:, 4 * g + h, SEQ:W],
                                     start=False, stop=True, skip_group_check=True)
                last.then_inc(pv_done, 1)

            def turn_out(r, s):
                if r.live(NB):
                    if s == 0:
                        pe.wait_ge(o_done, r.times(1, 1))
                        need(pe, h1_done, r.times(1, -1))
                    else:
                        pe.wait_ge(att_done, r.times(2, 1))
                    for g in range(3):
                        last = pe.transpose(x_ps[:, g * P:(g + 1) * P], o_sb[:, g, s * P:(s + 1) * P], k["eye32"][:])
                    last.then_inc(ot_done, 1)

            def turn_pack(r):
                if r.live(NB):
                    pe.wait_ge(lo_done, r.times(1, 1))
                    need(pe, chunks_done, r.times(1, 0))
                    for s in range(STEPS):
                        for c in range(3):
                            last = pe.transpose(c_ps[:, c, s * P:(s + 1) * P], pack[:, s, c * P:(c + 1) * P], k["eye16"][:])
                    last.then_inc(xt_done, 1)

            def project(r):
                if r.live(NB):
                    pe.wait_ge(chunks_done, r.times(1, 1))
                    if isinstance(r.turn, int) and r.c == NB - 1:
                        pe.wait_ge(h1_done, NB - 1)
                    else:
                        pe.wait_ge(att_done, r.times(2, 4))
                    for s in range(STEPS):
                        for c, (w, x) in enumerate(CHUNKS):
                            last = pe.matmul(x_ps[:, s * D:(s + 1) * D], chunks[:, x, s * P:(s + 1) * P], w_out[:, w, :],
                                             start=c == 0, stop=c == len(CHUNKS) - 1)
                    last.then_inc(wo_done, 1)

            def step(i):
                v, r = i.back(lag), i.back(turned_at)
                distances(i, (0, 1, 2))
                turn_out(r, 0)
                distances(i, (3,))
                turn_out(r, 1)
                distances(i, (4, 5, 6))
                turn(v, 0)
                distances(i, (7,))
                project(i.back(post))
                distances(i, (8,))
                turn(v, 1)
                values(v, 0)
                distances(i, (9,))
                turn_pack(r)
                turn(v, 2)
                values(v, 1)
                distances(i, (10, 11))
                values(v, 2)

            run_steps(pe, NB, 0, post, R, step)

        @block.vector
        def _(dve):
            nc.vector.memset(vals[:, :, STEPS * VROW:], 0.0).then_inc(padded, 1)

            def clamp(i, heads):
                if not i.live(NB):
                    return
                for h in heads:
                    dve.wait_ge(dist_mm, i.times(HEADS, h + 1))
                    if h == 0:
                        need(dve, pv_done, i.times(3, 3 - 3 * R))
                    nc.vector.tensor_scalar(dist[i.slot(R)][:, h, :], d_ps[h % 3][:, 0:W], 0.0, None,
                                            ALU.min).then_inc(clamped, 1)

            def keep_turned(v, g):
                if v.live(NB):
                    dve.wait_ge(turned, v.times(3, g + 1))
                    need(dve, pv_done, v.times(3, g - 1))
                    nc.vector.tensor_copy(e10[:, (v.slot(2) + g) % 2], t_ps).then_inc(e10_done, 1)

            def normalise(r, s):
                if r.live(NB):
                    dve.wait_ge(ot_done, r.times(2, s + 1))
                    heads = x_ps[:, 0:W].rearrange("p (h d) -> p h d", d=32)
                    nc.vector.reciprocal(recip[:, s, :], heads[:, :, HD]).then_inc(recip_done, 1)
                    dve.wait_ge(recip_done, r.times(2, s + 1))
                    if s == 0:
                        need(dve, lo_done, r.times(1, 0))
                    nc.vector.tensor_tensor(att[:, s, :].rearrange("p (h d) -> p h d", d=HD), heads[:, :, 0:HD],
                                            recip[:, s, :, None].to_broadcast([P, HEADS, HD]),
                                            ALU.mult).then_inc(att_done, 1)

            def add_rows(r):
                if r.live(NB):
                    a = r.slot(2)
                    dve.wait_ge(wo_done, r.times(1, 1))
                    dve.wait_ge(hb_in[a], r.use(2, 16, 16))
                    need(dve, h1_out[a], r.use(2, 16, 0))
                    nc.vector.scalar_tensor_tensor(out=h1[:, a], in0=x_ps[:, 0:STEPS * D].rearrange("p (s d) -> p s d", d=D),
                                                   scalar=inv, in1=hb[:, a], op0=ALU.mult, op1=ALU.add).then_inc(h1_done, 1)
                    dve.wait_ge(h1_done, r.times(1, 1))
                    need(dve, aggr_done, r.times(1, 0))
                    for s in range(STEPS):
                        last = nc.vector.bn_stats(stats[:, s, :], h1[:, a, s, :])
                    last.then_inc(stat_done, 1)

            def aggregate(r):
                if r.live(NB):
                    need(dve, stat_done, r.times(1, 1), apart)
                    for s in range(STEPS):
                        last = nc.vector.bn_aggr(moments[:, s, :], stats[:, s, :])
                    last.then_inc(aggr_done, 1)

            def keep_moments(r):
                if r.live(NB):
                    dve.wait_ge(aggr_done, r.times(1, 1))
                    into = mv[:, STEPS * r.c:STEPS * r.c + STEPS, :] if isinstance(r.turn, int) else \
                        mv[:, bass.ds(r.times(STEPS), STEPS), :]
                    nc.vector.tensor_copy(into, moments[:])

            def step(i):
                v, r, last = i.back(lag), i.back(turned_at), i.back(post)
                clamp(i, (0, 1, 2))
                normalise(r, 0)
                clamp(i, (3,))
                normalise(r, 1)
                clamp(i, (4, 5, 6))
                keep_turned(v, 0)
                clamp(i, (7, 8))
                keep_turned(v, 1)
                add_rows(last)
                clamp(i, (9,))
                keep_turned(v, 2)
                clamp(i, (10,))
                aggregate(last)
                clamp(i, (11,))
                keep_moments(last)

            moments = m.sb("moments", [P, STEPS, 2], F32)
            run_steps(dve, NB, 0, post, R, step)

        @block.scalar
        def _(act):
            def bulk(i, n):
                phase = i.slot(R)
                first = i.back(phase % group)
                t = first.back(group - 2 * (phase % (group // 2)) - n // 3)
                root = phase % group < group // 2
                g = n % 3
                if not t.live(NB):
                    return
                part = dist[t.slot(R)][:, 4 * g:4 * g + 4, :]
                if root:
                    act.wait_ge(clamped, t.times(HEADS, 4 * g + 4))
                    nc.scalar.activation(part, part, ACT.Sqrt, scale=-2.0).then_inc(rooted, 1)
                else:
                    act.wait_ge(rooted, t.times(3, g + 1))
                    nc.scalar.activation(part, part, ACT.Exp, scale=-float(HD) ** -0.5).then_inc(exped, 1)

            def keep_chunks(r):
                if r.live(NB):
                    act.wait_ge(xt_done, r.times(1, 1))
                    need(act, wo_done, r.times(1, 0))
                    nc.scalar.copy(chunks[:], c_ps[:, 0:3, :]).then_inc(chunks_done, 1)

            def keep_out(v):
                if v.live(NB):
                    act.wait_ge(pv_done, v.times(3, 3))
                    need(act, ot_done, v.times(2, 0))
                    nc.scalar.copy(o_sb[:], o_ps[:, 0:3, :]).then_inc(o_done, 1)

            def step(i):
                bulk(i, 0)
                keep_chunks(i.back(post))
                bulk(i, 1)
                keep_out(i.back(out))
                for n in range(2, 6):
                    bulk(i, n)

            run_steps(act, NB, 0, post, R, step)


TILES = 4
BLOCK = TILES * P


class FeedForward:

    def __init__(self, nc, m, nf, y_done):
        self.nc, self.nf, self.y_done = nc, nf, y_done
        self.chunks = m.sb("chunks", [P, 2, 3, BLOCK], F16)
        self.silu = m.sb("silu", [P, 2, BLOCK], F32)
        self.h_hi = m.sb("h_hi", [P, 3, BLOCK], F16)
        self.h_lo = m.sb("h_lo", [P, 3, BLOCK], F16)
        self.c_ps = m.ps("c_ps", [P, 4, BLOCK], F16)
        self.g_ps, self.u_ps, self.h_ps = m.bank("g_ps"), m.bank("u_ps"), m.bank("h_ps")
        self.y_ps = m.ps("y_ps", [P, 2, 512], F32)
        (self.turned, self.chunks_done, self.g_mm, self.u_mm, self.silu_done, self.h_done, self.hi_done,
         self.lo_done, self.down_mm) = (m.sem(x) for x in (
             "turned", "chunks_done", "g_mm", "u_mm", "silu_done", "h_done", "hi_done", "lo_done", "down_mm"))

    def y_tile(self, t):
        return self.y_ps[:, t // 2, t % 2 * D:(t % 2 + 1) * D]

    def turn(self, pe, b, n, rows, eye):
        if b.live(n):
            need(pe, self.chunks_done, b.times(1, 0))
            for t in range(TILES):
                for c in range(3):
                    last = pe.transpose(self.c_ps[:, c, t * P:(t + 1) * P], rows(b, t)[:, c * P:(c + 1) * P], eye[:])
            last.then_inc(self.turned, 1)

    def gate_up(self, pe, b, n, f, wg, wu):
        if not b.live(n):
            return
        nf, a = self.nf, b.slot(2)
        if f == 0:
            pe.wait_ge(self.chunks_done, b.times(1, 1))
        need(pe, self.silu_done, b.times(nf, f))
        for ps, w, done in ((self.g_ps, wg, self.g_mm), (self.u_ps, wu, self.u_mm)):
            if ps is self.u_ps:
                need(pe, self.h_done, b.times(nf, f))
            for c, (s, x) in enumerate(CHUNKS):
                last = pe.matmul(ps[:], w[:, s, f * P:(f + 1) * P], self.chunks[:, a, x, :],
                                 start=c == 0, stop=c == len(CHUNKS) - 1)
            last.then_inc(done, 1)

    def down(self, pe, b, n, f, wd):
        if not b.live(n):
            return
        pe.wait_ge(self.lo_done, b.times(self.nf, f + 1))
        if f == 0:
            need(pe, self.y_done, b.times(1, 0))
        for t in range(TILES):
            cols = slice(t * P, (t + 1) * P)
            for c, (h, part) in enumerate(((self.h_hi, 0), (self.h_hi, 1), (self.h_lo, 0))):
                last = pe.matmul(self.y_tile(t), h[:, f % 3, cols], wd[:, f, part, :],
                                 start=f == 0 and c == 0 and t % 2 == 0, stop=f == self.nf - 1 and c == 2,
                                 skip_group_check=True)
        last.then_inc(self.down_mm, 1)

    def keep_chunks(self, act, b, n):
        if b.live(n):
            act.wait_ge(self.turned, b.times(1, 1))
            need(act, self.u_mm, b.times(self.nf, -self.nf))
            self.nc.scalar.copy(self.chunks[:, b.slot(2)], self.c_ps[:, 0:3, :]).then_inc(self.chunks_done, 1)

    def activate(self, act, b, n, f):
        if not b.live(n):
            return
        nf, s = self.nf, (b.slot(2) * self.nf + f) % 2
        act.wait_ge(self.g_mm, b.times(nf, f + 1))
        need(act, self.h_done, b.times(nf, f - 1))
        self.nc.scalar.activation(self.silu[:, s], self.g_ps[:], ACT.Silu, scale=1.0 / SPLIT).then_inc(self.silu_done, 1)
        act.wait_ge(self.h_done, b.times(nf, f + 1))
        need(act, self.down_mm, b.times(nf, f - 2))
        self.nc.scalar.copy(self.h_hi[:, f % 3], self.h_ps[:]).then_inc(self.hi_done, 1)

    def hidden(self, dve, b, n, f):
        if not b.live(n):
            return
        nf, s = self.nf, (b.slot(2) * self.nf + f) % 2
        dve.wait_ge(self.silu_done, b.times(nf, f + 1))
        dve.wait_ge(self.u_mm, b.times(nf, f + 1))
        need(dve, self.lo_done, b.times(nf, f))
        self.nc.vector.scalar_tensor_tensor(out=self.h_ps[:], in0=self.u_ps[:], scalar=1.0 / SPLIT, in1=self.silu[:, s],
                                            op0=ALU.mult, op1=ALU.mult).then_inc(self.h_done, 1)

    def rest(self, dve, b, n, f):
        if b.live(n):
            nf = self.nf
            dve.wait_ge(self.hi_done, b.times(nf, f + 1))
            need(dve, self.down_mm, b.times(nf, f - 2))
            self.nc.vector.tensor_tensor(self.h_lo[:, f % 3], self.h_ps[:], self.h_hi[:, f % 3],
                                         ALU.subtract).then_inc(self.lo_done, 1)


def make_down(nc, k, name, src, wd, nf):
    with Mem(nc, name) as m:
        nat = m.sb("nat", [P, 2, nf * P], F32)
        parts = m.sb("parts", [P, 2, 2, nf * P], F16)
        turned = [m.bank(f"turned{i}", F16)[:, 0:2 * D].rearrange("p (c n) -> p c n", c=2) for i in range(2)]
        loaded, hi_done, lo_done, turned_done, kept = (m.sem(x) for x in ("loaded", "hi", "lo", "turned_done", "kept"))
        halves = ((0, P), (1, REST))
        block = m.block()

        @block.sync
        def _(sp):
            for half, n in halves:
                sp.dma_start(nat[0:n, half], src[half * P:half * P + n, :]).then_inc(loaded, 16)

        @block.scalar
        def _(act):
            act.wait_ge(loaded, 32)
            for half, n in halves:
                nc.scalar.activation(parts[0:n, half, 0], nat[0:n, half], ACT.Copy, scale=SPLIT).then_inc(hi_done, 1)

        @block.vector
        def _(dve):
            for half, n in halves:
                dve.wait_ge(hi_done, half + 1)
                nc.vector.scalar_tensor_tensor(out=parts[0:n, half, 1], in0=nat[0:n, half], scalar=SPLIT,
                                               in1=parts[0:n, half, 0], op0=ALU.mult, op1=ALU.subtract).then_inc(lo_done, 1)
            for f in range(nf):
                dve.wait_ge(turned_done, f + 1)
                nc.vector.tensor_copy(wd[:, f], turned[f % 2]).then_inc(kept, 1)

        @block.tensor
        def _(pe):
            pe.wait_ge(lo_done, 2)
            for f in range(nf):
                need(pe, kept, f - 1)
                for part in range(2):
                    for half, n in halves:
                        last = pe.transpose(turned[f % 2][:, part, half * P:half * P + n],
                                            parts[0:n, half, part, f * P:(f + 1) * P], k["eye16"][0:n, 0:n])
                last.then_inc(turned_done, 1)


def shared_expert(nc, k, dims, w, mv, scores, h1_dram, pack_dram, out_dram):
    NB, NT, E = dims["NB"], dims["NT"], dims["E"]
    NK = NT // TILES
    nf = dims["FS"] // P
    inv = 1.0 / SPLIT
    with Mem(nc, "shared") as m:
        out_done = m.sem("out")
        ff = FeedForward(nc, m, nf, out_done)
        std = m.sb("std", [P, NT], F32)
        rstd = m.sb("rstd", [P, NT], F32)
        mean_rstd = m.sb("mean_rstd", [P, 2, TILES, 2], F32)
        h1 = m.sb("h1", [P, 3, TILES, D], F32)
        xn = m.sb("xn", [P, TILES, D], F32)
        pack = m.sb("pack", [P, 2, TILES, PACK], F16)
        out = m.sb("out", [P, 2, TILES, D], F32)
        l_ps = m.bank("l_ps")[:, 0:TILES * E].rearrange("p (t e) -> p t e", e=E)
        std_done, rstd_done, picked, xn_done, split_done, packed, logits_mm, logits_done, sig_done = (
            m.sem(x) for x in ("std", "rstd", "picked", "xn", "split", "packed", "logits_mm", "logits", "sig"))
        h1_in, pack_out, base_out = m.sems("h1_in", 3), m.sems("pack_out", 2), m.sems("base_out", 2)
        score_out = m.sem("score_out")
        block = m.block()
        PERIOD = 6

        def seqs(dram, b):
            q = BLOCK // SEQ
            part = dram[q * b.c:q * b.c + q] if isinstance(b.turn, int) else dram[bass.ds(b.times(q), q)]
            return part.rearrange("q p s d -> p q (s d)")

        def rows(dram, b):
            part = dram[BLOCK * b.c:BLOCK * b.c + BLOCK, :] if isinstance(b.turn, int) else dram[bass.ds(b.times(BLOCK), BLOCK), :]
            return part.rearrange("(t p) d -> p t d", p=P)

        @block.sync
        def _(sp):
            def step(i):
                t = i.back(-1)
                if t.live(NK):
                    need(sp, out_done, t.times(1, -2))
                    sp.dma_start(h1[:, t.slot(3)].rearrange("p (q s) d -> p q (s d)", s=STEPS),
                                 seqs(h1_dram, t)).then_inc(h1_in[t.slot(3)], 16)
                if i.live(NK):
                    sp.wait_ge(packed, i.times(1, 1))
                    sp.dma_start(rows(pack_dram[:, 0:PACK // 2], i), pack[:, i.slot(2)].bitcast(U32)).then_inc(pack_out[i.slot(2)], 16)
                t = i.back(2)
                if t.live(NK):
                    sp.wait_ge(out_done, t.times(1, 1))
                    sp.dma_start(rows(out_dram, t), out[:, t.slot(2)]).then_inc(base_out[t.slot(2)], 16)

            run_steps(sp, NK, 1, 2, PERIOD, step)
            sp.wait_ge(sig_done, 1)
            for t in range(0, NT, TILES):
                sp.dma_start(pack_dram[t * P:(t + TILES) * P, PACK // 2:PACK // 2 + E].rearrange("(t p) c -> p t c", p=P),
                             scores[:, t:t + TILES, :].bitcast(U32)).then_inc(score_out, 16)
            sp.wait_ge(score_out, 16 * (NT // TILES))
            for a in range(2):
                uses = (NK - a + 1) // 2
                sp.wait_ge(pack_out[a], 16 * uses)
                sp.wait_ge(base_out[a], 16 * uses)


        @block.vector
        def _(dve):
            dve.wait_ge(std_done, 1)
            nc.vector.reciprocal(rstd[:], std[:]).then_inc(rstd_done, 1)
            dve.wait_ge(rstd_done, 1)

            def normalise(i):
                if not i.live(NK):
                    return
                tiles = slice(TILES * i.c, TILES * i.c + TILES) if isinstance(i.turn, int) else bass.ds(i.times(TILES), TILES)
                a = i.slot(2)
                need(dve, xn_done, i.times(1, -1))
                nc.vector.tensor_copy(mean_rstd[:, a, :, 0], mv[:, tiles, 0])
                nc.vector.tensor_copy(mean_rstd[:, a, :, 1], rstd[:, tiles]).then_inc(picked, 1)
                dve.wait_ge(picked, i.times(1, 1))
                dve.wait_ge(h1_in[i.slot(3)], i.use(3, 16, 16))
                need(dve, packed, i.times(1, 0))
                for t in range(TILES):
                    last = nc.vector.tensor_scalar(xn[:, t, :], h1[:, i.slot(3), t, :], mean_rstd[:, a, t, 0:1],
                                                   mean_rstd[:, a, t, 1:2], ALU.subtract, ALU.mult)
                last.then_inc(xn_done, 1)

            def keep_logits(b):
                if b.live(NK):
                    dve.wait_ge(logits_mm, b.times(1, 1))
                    tiles = slice(TILES * b.c, TILES * b.c + TILES) if isinstance(b.turn, int) else bass.ds(b.times(TILES), TILES)
                    nc.vector.tensor_scalar(scores[:, tiles, :], l_ps, inv, None, ALU.mult).then_inc(logits_done, 1)

            def add(b):
                if b.live(NK):
                    dve.wait_ge(ff.down_mm, b.times(nf, nf))
                    need(dve, base_out[b.slot(2)], b.use(2, 16))
                    for half in range(2):
                        two = slice(2 * half, 2 * half + 2)
                        last = nc.vector.scalar_tensor_tensor(
                            out=out[:, b.slot(2), two, :].rearrange("p t d -> p (t d)"), in0=ff.y_ps[:, half, 0:2 * D], scalar=inv,
                            in1=h1[:, b.slot(3), two, :].rearrange("p t d -> p (t d)"), op0=ALU.mult, op1=ALU.add)
                    last.then_inc(out_done, 1)

            def step(i):
                b, before = i.back(1), i.back(2)
                ff.hidden(dve, b, NK, 0)
                normalise(i)
                ff.rest(dve, b, NK, 0)
                add(before)
                for f in range(1, nf):
                    ff.hidden(dve, b, NK, f)
                    if f == 1:
                        keep_logits(b)
                    ff.rest(dve, b, NK, f)

            run_steps(dve, NK, 0, 2, PERIOD, step)

        @block.scalar
        def _(act):
            nc.scalar.activation(std[:], mv[:, :, 1], ACT.Sqrt, bias=k["eps"][:]).then_inc(std_done, 1)

            def split(i):
                if i.live(NK):
                    a = i.slot(2)
                    act.wait_ge(xn_done, i.times(1, 1))
                    need(act, ff.turned, i.times(1, -1))
                    need(act, pack_out[a], i.use(2, 16))
                    nc.scalar.copy(pack[:, a, :, 0:D], xn[:]).then_inc(split_done, 1)

            def step(i):
                b = i.back(1)
                ff.activate(act, b, NK, 0)
                split(i)
                for f in range(1, nf - 1):
                    ff.activate(act, b, NK, f)
                ff.keep_chunks(act, i, NK)
                ff.activate(act, b, NK, nf - 1)

            run_steps(act, NK, 0, 2, PERIOD, step)
            act.wait_ge(logits_done, NK)
            nc.scalar.activation(scores[:], scores[:], ACT.Sigmoid).then_inc(sig_done, 1)

        @block.gpsimd
        def _(pool):
            def step(i):
                if i.live(NK):
                    a = i.slot(2)
                    pool.wait_ge(split_done, i.times(1, 1))
                    nc.gpsimd.tensor_tensor(pack[:, a, :, D:2 * P], xn[:, :, P:D], pack[:, a, :, P:D], ALU.subtract)
                    nc.gpsimd.tensor_tensor(pack[:, a, :, 2 * P:PACK], xn[:, :, 0:P], pack[:, a, :, 0:P],
                                            ALU.subtract).then_inc(packed, 1)

            run_steps(pool, NK, 0, 2, PERIOD, step)

        @block.tensor
        def _(pe):
            def logits(b):
                if b.live(NK):
                    need(pe, logits_done, b.times(1, 0))
                    for t in range(TILES):
                        for c, (s, x) in enumerate(CHUNKS):
                            last = pe.matmul(l_ps[:, t, :], ff.chunks[:, b.slot(2), x, t * P:(t + 1) * P], w["gate"][:, s, :],
                                             start=c == 0, stop=c == len(CHUNKS) - 1)
                    last.then_inc(logits_mm, 1)

            def step(i):
                b, before = i.back(1), i.back(2)
                ff.gate_up(pe, b, NK, 0, w["sg"], w["su"])
                ff.down(pe, before, NK, nf - 1, w["sd"])
                ff.gate_up(pe, b, NK, 1, w["sg"], w["su"])
                logits(b)
                ff.down(pe, b, NK, 0, w["sd"])
                if i.live(NK):
                    pe.wait_ge(packed, i.times(1, 1))
                ff.turn(pe, i, NK, lambda t, s: pack[:, t.slot(2), s, :], k["eye16"])
                for f in range(2, nf):
                    ff.gate_up(pe, b, NK, f, w["sg"], w["su"])
                    ff.down(pe, b, NK, f - 1, w["sd"])

            run_steps(pe, NK, 0, 2, PERIOD, step)


def choose_tokens(nc, k, dims, scores, counts, before, upto):
    NT, E, cap = dims["NT"], dims["E"], dims["cap"]
    SUB = P // E
    G = NT // SUB
    PER = 8
    BITS = 30
    with Mem(nc, "choose") as m:
        side = m.sb("side", [P, G, P], F32)
        mask = m.sb("mask", [P, G, P], F16)
        above, equal = m.sb("above", [P, G, P], F16), m.sb("equal", [P, G, P], F16)
        above_t, equal_t = m.sb("above_t", [P, NT, E], F16), m.sb("equal_t", [P, NT, E], F16)
        chosen = m.sb("chosen", [P, NT, E], F16)
        spread = m.sb("spread", [P, NT, E], F16)
        tiled_eye = m.sb("tiled_eye", [E, SUB, E], F32)
        same = m.sb("same", [P, P], F32)
        less, up = m.sb("less", [P, P], F16), m.sb("up", [P, P], F16)
        ones, ones32 = m.sb("ones", [P, P], F16), m.sb("ones32", [P, P], F32)
        missing_rows = m.sb("missing_rows", [P, P], F32)
        missing_sb = m.sb("missing_sb", [P, E], F32)
        totals, totals16 = m.sb("totals", [P, E], F32), m.sb("totals16", [P, E], F16)
        count, missing, bit, next_bit = (m.sb(x, [P, 1], F32) for x in ("count", "missing", "bit", "next_bit"))
        delta, found, candidate, next_int = (m.sb(x, [P, 1], I32) for x in ("delta", "found", "candidate", "next_int"))
        wide = [m.bank(f"wide{i}") for i in range(4)]
        small, other = m.bank("small"), m.bank("other")
        turn_ps = [m.bank(f"turn{i}") for i in range(2)]
        (cleared, triangles, sided, side_done, same_mm, same_done, counted, halved, count_mm, delta_done, found_done,
         moved, masks, missing_done, rows_done, back, kept, tot_mm, tot_done, spread_done, rank_mm, ranked, chosen_a,
         chosen_b, count_in, counts_done, tots, before_mm, end, need_mm, need_done) = (m.sem(x) for x in (
             "cleared", "triangles", "sided", "side_done", "same_mm", "same_done", "counted", "halved", "count_mm",
             "delta_done", "found_done", "moved", "masks", "missing_done", "rows_done", "back", "kept", "tot_mm",
             "tot_done", "spread_done", "rank_mm", "ranked", "chosen_a", "chosen_b", "count_in", "counts_done", "tots",
             "before_mm", "end", "need_mm", "need_done"))
        WN = 512 // E
        NW = -(-NT // WN)
        EW = 512 // P
        block = m.block()

        @block.gpsimd
        def _(pool):
            nc.gpsimd.memset(less[:], 1.0).then_inc(cleared, 1)
            nc.gpsimd.memset(up[:], 1.0).then_inc(cleared, 1)
            pool.wait_ge(cleared, 2)
            for tri, base in ((less, -1), (up, 0)):
                nc.gpsimd.affine_select(out=tri[:], in_=tri[:], compare_op=ALU.is_ge, fill=0.0, base=base,
                                        pattern=[[1, P]], channel_multiplier=-1).then_inc(triangles, 1)

        @block.vector
        def _(dve):
            nc.vector.memset(ones[:], 1.0)
            nc.vector.memset(ones32[:], 1.0)
            nc.vector.memset(found[:], 0)
            nc.vector.memset(candidate[:], 1 << (BITS - 1)).then_inc(found_done, 1)
            nc.vector.memset(bit[:], 2.0 ** (BITS - 1)).then_inc(moved, 1)
            nc.vector.tensor_copy(tiled_eye[:], k["eye32"][0:E, None, 0:E].to_broadcast([E, SUB, E])).then_inc(same_done, 1)
            for g in range(0, G, 4):
                n = min(4, G - g)
                dve.wait_ge(sided, g // 4 + 1)
                nc.vector.tensor_copy(side[:, g:g + n, :].rearrange("p g n -> p (g n)"),
                                      turn_ps[g // 4 % 2][:, 0:n * P]).then_inc(side_done, 1)
            dve.wait_ge(same_mm, 1)
            nc.vector.tensor_copy(same[:], other[:, 0:P]).then_inc(same_done, 1)
            dve.wait_ge(side_done, -(-G // 4))

            with dve.Fori(0, BITS) as i:
                dve.wait_ge(found_done, i * 2 + 1)
                nc.vector.tensor_scalar(mask[:], side[:], candidate[:].bitcast(F32), None, ALU.is_ge, ALU.add,
                                        accum_out=count[:]).then_inc(counted, 1)
                dve.wait_ge(moved, i + 1)
                nc.vector.tensor_scalar(next_bit[:], bit[:], 0.5, None, ALU.mult).then_inc(halved, 1)
                dve.wait_ge(halved, i * 2 + 1)
                nc.vector.tensor_copy(next_int[:], next_bit[:]).then_inc(halved, 1)
                dve.wait_ge(count_mm, i + 1)
                nc.vector.tensor_scalar(delta[:], small[:, 0:1], cap - 0.5, bit[:], ALU.is_ge, ALU.mult).then_inc(delta_done, 1)
                dve.wait_ge(delta_done, i + 1)
                nc.vector.tensor_tensor(found[:], found[:], delta[:], ALU.bitwise_or).then_inc(found_done, 1)
                nc.vector.tensor_copy(bit[:], next_bit[:]).then_inc(moved, 1)
                dve.wait_ge(found_done, i * 2 + 2)
                dve.wait_ge(halved, i * 2 + 2)
                nc.vector.tensor_tensor(candidate[:], found[:], next_int[:], ALU.bitwise_or).then_inc(found_done, 1)

            dve.wait_ge(found_done, 2 * BITS + 1)
            limit = found[:].bitcast(F32)
            nc.vector.tensor_scalar(above[:], side[:], limit, None, ALU.is_gt, ALU.add, accum_out=count[:]).then_inc(counted, 1)
            nc.vector.tensor_scalar(equal[:], side[:], limit, None, ALU.is_equal).then_inc(masks, 1)
            dve.wait_ge(count_mm, BITS + 1)
            nc.vector.tensor_scalar(missing[:], small[:, 0:1], -1.0, float(cap), ALU.mult, ALU.add).then_inc(missing_done, 1)
            dve.wait_ge(missing_done, 1)
            nc.vector.tensor_scalar(missing_rows[:], ones32[:], missing[:], None, ALU.mult).then_inc(rows_done, 1)
            dve.wait_ge(need_mm, 1)
            nc.vector.tensor_copy(missing_sb[:], small[:, 32:32 + E]).then_inc(need_done, 1)
            dve.wait_ge(tot_mm, 1)
            nc.vector.tensor_copy(totals16[0:NT, :], small[0:NT, 64:64 + E]).then_inc(tot_done, 1)
            dve.wait_ge(tot_done, 1)
            dve.wait_ge(triangles, 2)
            nc.vector.tensor_tensor(spread[0:NT], totals16[0:NT, None, :].to_broadcast([NT, NT, E]),
                                    less[0:NT, 0:NT, None].to_broadcast([NT, NT, E]), ALU.mult).then_inc(spread_done, 1)
            dve.wait_ge(rank_mm, 1)
            dve.wait_ge(need_done, 1)
            for w in range(NW):
                n = min(WN, NT - w * WN)
                nc.vector.tensor_tensor(chosen[:, w * WN:w * WN + n, :], wide[w][:, 0:n * E].rearrange("p (t e) -> p t e", e=E),
                                        missing_sb[:, None, :].to_broadcast([P, n, E]), ALU.is_lt).then_inc(ranked, 1)
            dve.wait_ge(ranked, NW)
            nc.vector.tensor_tensor(chosen[:], chosen[:], equal_t[:], ALU.mult).then_inc(chosen_a, 1)
            dve.wait_ge(chosen_a, 1)
            nc.vector.tensor_tensor(chosen[:], chosen[:], above_t[:], ALU.add).then_inc(chosen_b, 1)
            dve.wait_ge(count_in, 1)
            for w in range(E // EW):
                nc.vector.tensor_copy(counts[0:NT, w * EW:(w + 1) * EW, :],
                                      wide[w][0:NT, :].rearrange("p (e n) -> p e n", n=P)).then_inc(counts_done, 1)
            dve.wait_ge(counts_done, E // EW)
            nc.vector.tensor_copy(totals16[0:NT, :], counts[0:NT, :, P - 1]).then_inc(tots, 1)
            dve.wait_ge(before_mm, 1)
            nc.vector.tensor_copy(before[0:NT, :], small[0:NT, 96:96 + E]).then_inc(end, 1)
            dve.wait_ge(end, 1)
            nc.vector.tensor_tensor(upto[0:NT, :], before[0:NT, :], totals16[0:NT, :], ALU.add).then_inc(end, 1)

        @block.scalar
        def _(act):
            for n in range(2 * -(-G // PER)):
                which, g = n % 2, n // 2 * PER
                groups = min(PER, G - g)
                act.wait_ge(back, n + 1)
                nc.scalar.copy((above_t, equal_t)[which][:, g * SUB:(g + groups) * SUB, :].rearrange("p t e -> p (t e)"),
                               turn_ps[n % 2][:].bitcast(F16)[:, 0:groups * P]).then_inc(kept, 1)

        @block.tensor
        def _(pe):
            for g in range(0, G, 4):
                need(pe, side_done, g // 4 - 1)
                for j in range(min(4, G - g)):
                    tiles = scores[:, (g + j) * SUB:(g + j + 1) * SUB, :].rearrange("p t e -> p (t e)")
                    last = pe.transpose(turn_ps[g // 4 % 2][:, j * P:(j + 1) * P], tiles, k["eye32"][:])
                last.then_inc(sided, 1)
            pe.wait_ge(same_done, 1)
            eyes = tiled_eye[:].rearrange("a s e -> a (s e)")
            pe.matmul(other[:, 0:P], eyes, eyes, start=True, stop=True).then_inc(same_mm, 1)
            pe.wait_ge(same_done, 2)
            with pe.Fori(0, BITS) as i:
                pe.wait_ge(counted, i + 1)
                pe.matmul(small[:, 0:1], same[:], count[:], start=True, stop=True).then_inc(count_mm, 1)
            pe.wait_ge(counted, BITS + 1)
            pe.matmul(small[:, 0:1], same[:], count[:], start=True, stop=True).then_inc(count_mm, 1)
            pe.wait_ge(rows_done, 1)
            pe.matmul(small[:, 32:32 + E], missing_rows[:], k["eye32"][:, 0:E], start=True, stop=True).then_inc(need_mm, 1)
            pe.wait_ge(masks, 1)
            pe.wait_ge(side_done, -(-G // 4))
            for n in range(2 * -(-G // PER)):
                which, g = n % 2, n // 2 * PER
                need(pe, kept, n - 1)
                for j in range(min(PER, G - g)):
                    last = pe.transpose(turn_ps[n % 2][:].bitcast(F16)[:, j * P:(j + 1) * P], (above, equal)[which][:, g + j, :],
                                        k["eye16"][:])
                last.then_inc(back, 1)
            pe.wait_ge(kept, 2 * -(-G // PER))
            pe.wait_ge(need_done, 1)
            for e in range(E):
                last = pe.matmul(small[0:NT, 64 + e:65 + e], equal_t[:, :, e], ones[:, 0:1], start=True, stop=True)
            last.then_inc(tot_mm, 1)
            pe.wait_ge(spread_done, 1)
            for w in range(NW):
                n = min(WN, NT - w * WN)
                tiles = slice(w * WN, w * WN + n)
                pe.matmul(wide[w][:, 0:n * E], less[:], equal_t[:, tiles, :].rearrange("p t e -> p (t e)"),
                          start=True, stop=False)
                last = pe.matmul(wide[w][:, 0:n * E], ones[0:NT, :], spread[0:NT, tiles, :].rearrange("p t e -> p (t e)"),
                                 start=False, stop=True)
            last.then_inc(rank_mm, 1)
            pe.wait_ge(chosen_b, 1)
            for e in range(E):
                last = pe.matmul(wide[e // EW][0:NT, e % EW * P:(e % EW + 1) * P], chosen[:, :, e], up[:], start=True, stop=True)
            last.then_inc(count_in, 1)
            pe.wait_ge(tots, 1)
            pe.matmul(small[0:NT, 96:96 + E], less[0:NT, 0:NT], totals16[0:NT, :], start=True, stop=True).then_inc(before_mm, 1)


def experts(nc, k, dims, counts, before, upto, wg_dram, wu_dram, wd_dram, pack_dram, out_dram):
    NT, E, cap = dims["NT"], dims["E"], dims["cap"]
    nf = dims["F"] // P
    per = cap // BLOCK
    n = E * per
    ZT = cap // P
    inv = 1.0 / SPLIT
    ROW = PACK // 2 + E
    assert per == 4 and nf == 6 and cap <= 2048 and NT <= P
    PERIOD = 2 * per
    LEAD = per - 1

    pieces = {q: [p for p in range(nf) if p * per // nf == q] for q in range(per)}
    jobs, order = {}, {}
    for q in range(per):
        if (q - LEAD) % per == per - 2:
            jobs[q] = {1: ("rows", 0), 3: ("rows", 1), 5: ("rows", 2), 7: ("rows", 3), 9: ("ids", 0),
                       10: ("first", pieces[q][0]), 11: ("second", pieces[q][0])}
            assert len(pieces[q]) == 1
        else:
            places = ((2, 4), (8, 10))
            jobs[q] = {place: (kind, p) for p, at in zip(pieces[q], places)
                       for place, kind in zip(at, ("first", "second"))}
        for place in sorted(jobs[q]):
            order[q, place] = len(order)
    SHARES = len(order)
    IDS_AT = order[(LEAD + per - 2) % per, 9]

    with Mem(nc, "experts") as m:
        y_done = m.sem("y_done")
        ff = FeedForward(nc, m, nf, y_done)
        wg, wu = m.sb("wg", [P, 2, 4, nf * P], F16), m.sb("wu", [P, 2, 4, nf * P], F16)
        wd = m.sb("wd", [P, 2, nf, 2, D], F16)
        nat = m.sb("nat", [P, 2, nf, D], F32)
        nat_d = m.sb("nat_d", [P, 2, nf * P], F32)
        parts = m.sb("parts", [P, 2, 2, 4 * P], F16)
        parts_d = m.sb("parts_d", [P, 2, 2, 2, P], F16)
        slots = m.sb("slots", [P, cap], F32)
        limits = m.sb("limits", [P, 2], F32)
        reach = m.sb("reach", [P, P], F16)
        past = m.sb("past", [P, cap], F16)
        own = m.sb("own", [P, cap], F16)
        earlier = m.sb("earlier", [P, cap], F16)
        hundred, one = m.sb("hundred", [P, 1], F16), m.sb("one", [P, 1], F16)
        ids = m.sb("ids", [P, 2, ZT], U32)
        rows = m.sb("rows", [P, 2, TILES, ROW], U32)
        score = m.sb("score", [P, 4, TILES], F32)
        y = m.sb("y", [P, 2, TILES, D], F32)
        shared = m.bank("shared")
        (w_hi, w_lo, w_twice, w_first, w_second, kept, set_up, nat_in, limits_done, reach_done, past_done,
         own_done, rows_mm, earlier_done, ids_mm, score_done, apart) = (m.sem(x) for x in (
             "w_hi", "w_lo", "w_twice", "w_first", "w_second", "kept", "set_up", "nat_in",
             "limits", "reach", "past", "own", "rows_mm", "earlier", "ids_mm", "score", "apart"))
        got, added = m.sems("got", 2), m.sems("added", 2)
        halves = ((0, P), (1, REST))
        block = m.block()

        def expert(t):
            return t.use(per)

        def column(tensor, t):
            return tensor[:, t.c // per:t.c // per + 1] if isinstance(t.turn, int) else tensor[:, bass.ds(expert(t), 1)]

        def places(i, do):
            t = i.back(-LEAD)
            q = t.slot(per)

            def at(place):
                if t.live(n) and place in jobs[q]:
                    kind, what = jobs[q][place]
                    do(t, kind, what, t.use(per, SHARES, order[q, place]))
            return at

        def piece(t, p, plus=0):
            return t.use(per, nf, p + plus)

        @block.sync
        def _(sp):
            def load(t):
                if t.live(n) and t.slot(per) == 0:
                    need(sp, w_lo, t.use(per, nf, 0))
                    e = t.c // per if isinstance(t.turn, int) else expert(t)
                    for j, w in enumerate((wg_dram, wu_dram)):
                        sp.dma_start(nat[:, j], w[e].rearrange("(f p) d -> p f d", p=P)).then_inc(nat_in, 16)
                    for half, rows_n in halves:
                        sp.dma_start(nat_d[0:rows_n, half], wd_dram[e][half * P:half * P + rows_n, :]).then_inc(nat_in, 16)

            run_steps(sp, n, LEAD + 1, 0, PERIOD, lambda i: load(i.back(-LEAD - 1)))

        @block.gpsimd
        def _(pool):
            nc.gpsimd.iota(slots[:], pattern=[[1, cap]], base=0, channel_multiplier=0,
                           allow_small_or_imprecise_dtypes=True).then_inc(set_up, 1)

            def step(i):
                t = i.back(-1)
                if t.live(n):
                    a, q = t.slot(2), t.slot(per)
                    if q == 0:
                        need(pool, kept, t.use(per, SHARES, IDS_AT + 1), apart)
                    need(pool, ff.turned, t.times(1, -1))
                    need(pool, score_done, t.times(1, -1), apart)
                    for s in range(TILES):
                        z = q * TILES + s
                        nc.gpsimd.indirect_dma_start(
                            out=rows[:, a, s, :], out_offset=None, in_=pack_dram,
                            in_offset=bass.IndirectOffsetOnAxis(ap=ids[:, t.slot(PERIOD) // per, z:z + 1], axis=0)
                        ).then_inc(got[a], 16)
                t = i.back(-LEAD)
                if t.live(n):
                    for p in pieces[t.slot(per)]:
                        need(pool, w_lo, piece(t, p, 1), apart)
                        for c in (0, 2 * P):
                            last = nc.gpsimd.tensor_copy(parts[:, p % 2, :, c + D:c + 2 * P], parts[:, p % 2, :, c + P:c + D])
                        last.then_inc(w_twice, 1)
                t = i.back(2)
                if t.live(n):
                    a, q = t.slot(2), t.slot(per)
                    if q == 0:
                        for s in range(2):
                            need(pool, added[s], t.use(per, 16 * TILES * per // 2))
                    need(pool, y_done, t.times(1, 1), apart)
                    for s in range(TILES):
                        z = q * TILES + s
                        nc.gpsimd.indirect_dma_start(
                            out=out_dram, in_=y[:, a, s, :], in_offset=None, compute_op=ALU.add,
                            out_offset=bass.IndirectOffsetOnAxis(ap=ids[:, t.slot(PERIOD) // per, z:z + 1], axis=0)
                        ).then_inc(added[a], 16)

            run_steps(pool, n, LEAD, 2, PERIOD, step)
            for s in range(2):
                pool.wait_ge(added[s], 16 * TILES * n // 2)

        @block.scalar
        def _(act):
            def split(i, which):
                t = i.back(-LEAD)
                if not t.live(n) or which >= len(pieces[t.slot(per)]):
                    return
                p = pieces[t.slot(per)][which]
                if p == 0:
                    act.wait_ge(nat_in, t.use(per, 64, 64))
                need(act, w_second, piece(t, p, -1))
                nc.scalar.activation(parts[:, p % 2, :, 0:D], nat[:, :, p, :], ACT.Copy, scale=SPLIT)
                for half, rows_n in halves:
                    last = nc.scalar.activation(parts_d[0:rows_n, p % 2, half, 0, :], nat_d[0:rows_n, half, p * P:(p + 1) * P],
                                                ACT.Copy, scale=SPLIT)
                last.then_inc(w_hi, 1)

            def step(i):
                b = i.back(1)
                split(i, 0)
                ff.activate(act, b, n, 0)
                ff.activate(act, b, n, 1)
                split(i, 1)
                ff.activate(act, b, n, 2)
                ff.activate(act, b, n, 3)
                ff.keep_chunks(act, i, n)
                ff.activate(act, b, n, 4)
                ff.activate(act, b, n, 5)

            run_steps(act, n, LEAD, 2, PERIOD, step)

        @block.vector
        def _(dve):
            nc.vector.memset(hundred[:], float(P))
            nc.vector.memset(one[:], 1.0).then_inc(set_up, 1)
            dve.wait_ge(set_up, 2)

            def split(i, which):
                t = i.back(-LEAD)
                if not t.live(n) or which >= len(pieces[t.slot(per)]):
                    return
                p = pieces[t.slot(per)][which]
                dve.wait_ge(w_hi, piece(t, p, 1))
                nc.vector.scalar_tensor_tensor(out=parts[:, p % 2, :, 2 * P:2 * P + D], in0=nat[:, :, p, :], scalar=SPLIT,
                                               in1=parts[:, p % 2, :, 0:D], op0=ALU.mult, op1=ALU.subtract)
                for half, rows_n in halves:
                    last = nc.vector.scalar_tensor_tensor(
                        out=parts_d[0:rows_n, p % 2, half, 1, :], in0=nat_d[0:rows_n, half, p * P:(p + 1) * P], scalar=SPLIT,
                        in1=parts_d[0:rows_n, p % 2, half, 0, :], op0=ALU.mult, op1=ALU.subtract)
                last.then_inc(w_lo, 1)

            def prepare_ids(i):
                t = i.back(-2)
                if not t.live(n) or t.slot(per) != 0:
                    return
                nc.vector.tensor_copy(limits[0:NT, 0:1], column(before, t)[0:NT])
                nc.vector.tensor_copy(limits[0:NT, 1:2], column(upto, t)[0:NT]).then_inc(limits_done, 1)
                dve.wait_ge(limits_done, t.use(per, 1, 1))
                need(dve, ids_mm, t.use(per, 1, 0))
                mine = counts[0:NT, t.c // per, :] if isinstance(t.turn, int) else counts[0:NT, bass.ds(expert(t), 1), :]
                nc.vector.tensor_scalar(reach[0:NT, :], mine, limits[0:NT, 0:1], None, ALU.add).then_inc(reach_done, 1)
                nc.vector.tensor_scalar(past[0:NT, :], slots[0:NT, :], limits[0:NT, 1:2], None, ALU.is_ge).then_inc(past_done, 1)
                dve.wait_ge(past_done, t.use(per, 1, 1))
                nc.vector.scalar_tensor_tensor(out=own[0:NT, :], in0=slots[0:NT, :], scalar=limits[0:NT, 0:1],
                                               in1=past[0:NT, :], op0=ALU.is_ge, op1=ALU.subtract).then_inc(own_done, 1)

            def job(t, kind, what, share):
                parity = t.slot(PERIOD) // per
                if kind == "first":
                    dve.wait_ge(w_first, piece(t, what, 1))
                    if what == 0:
                        need(dve, ff.down_mm, t.use(per, nf * per, -nf * per))
                    cols = slice(what * P, (what + 1) * P)
                    turned = shared[:].bitcast(F16).rearrange("p (j c n) -> p j c n", j=2, c=4)
                    nc.vector.tensor_copy(wg[:, parity, :, cols], turned[:, 0])
                    nc.vector.tensor_copy(wu[:, parity, :, cols], turned[:, 1]).then_inc(kept, 1)
                if kind == "second":
                    dve.wait_ge(w_second, piece(t, what, 1))
                    nc.vector.tensor_copy(wd[:, parity, what], shared[:].bitcast(F16)[:, 0:2 * D].rearrange(
                        "p (c n) -> p c n", c=2)).then_inc(kept, 1)
                if kind == "rows":
                    dve.wait_ge(rows_mm, t.use(per, 4, what + 1))
                    cols = slice(what * 512, (what + 1) * 512)
                    nc.vector.tensor_tensor(earlier[:, cols], shared[:], slots[:, cols], ALU.is_le).then_inc(kept, 1)
                if kind == "ids":
                    dve.wait_ge(ids_mm, t.use(per, 1, 1))
                    for s in range(2):
                        need(dve, added[s], t.use(per, 16 * TILES * per // 2, -16 * TILES * per // 2))
                    nc.vector.tensor_copy(ids[:, parity, :], shared[:, 0:ZT]).then_inc(kept, 1)

            def keep_scores(t):
                if t.live(n):
                    need(dve, got[t.slot(2)], t.use(2, 16 * TILES, 16 * TILES), apart)
                    words = rows[:, t.slot(2)].bitcast(F32)
                    at = PACK // 2
                    mine = words[:, :, at + t.c // per] if isinstance(t.turn, int) else words[:, :, bass.ds(expert(t) + at, 1)]
                    nc.vector.tensor_copy(score[:, t.slot(4), :], mine).then_inc(score_done, 1)

            def scale(t):
                if t.live(n):
                    a = t.slot(2)
                    dve.wait_ge(ff.down_mm, t.times(nf, nf))
                    need(dve, added[a], t.use(2, 16 * TILES))
                    for s in range(TILES):
                        last = nc.vector.tensor_scalar(y[:, a, s, :], ff.y_tile(s), score[:, t.slot(4), s:s + 1], inv,
                                                       ALU.mult, ALU.mult)
                    last.then_inc(y_done, 1)

            def step(i):
                b, last = i.back(1), i.back(2)
                at = places(i, job)
                prepare_ids(i)
                split(i, 0)
                for f in range(nf):
                    ff.hidden(dve, b, n, f)
                    if f == 0:
                        ff.rest(dve, b, n, f)
                        scale(last)
                    if f == 2:
                        split(i, 1)
                    if f == 3:
                        keep_scores(i)
                    at(2 * f)
                    if f:
                        ff.rest(dve, b, n, f)
                    at(2 * f + 1)

            run_steps(dve, n, LEAD, 2, PERIOD, step)

        @block.tensor
        def _(pe):
            pe.wait_ge(set_up, 2)

            def job(t, kind, what, share):
                need(pe, kept, share)
                if kind == "first":
                    pe.wait_ge(w_twice, piece(t, what, 1))
                    turned = shared[:].bitcast(F16).rearrange("p (j c n) -> p j c n", j=2, c=4)
                    for j in range(2):
                        for c in range(4):
                            last = pe.transpose(turned[:, j, c, :], parts[:, what % 2, j, c * P:(c + 1) * P], k["eye16"][:])
                    last.then_inc(w_first, 1)
                if kind == "second":
                    turned = shared[:].bitcast(F16)[:, 0:2 * D].rearrange("p (c n) -> p c n", c=2)
                    for part in range(2):
                        for half, rows_n in halves:
                            last = pe.transpose(turned[:, part, half * P:half * P + rows_n],
                                                parts_d[0:rows_n, what % 2, half, part, :], k["eye16"][0:rows_n, 0:rows_n])
                    last.then_inc(w_second, 1)
                if kind == "rows":
                    if what == 0:
                        pe.wait_ge(own_done, t.use(per, 1, 1))
                    pe.matmul(shared[:], reach[0:NT, :], own[0:NT, what * 512:(what + 1) * 512],
                              start=True, stop=True).then_inc(rows_mm, 1)
                if kind == "ids":
                    for z in range(ZT):
                        cols = slice(z * P, (z + 1) * P)
                        pe.matmul(shared[:, z:z + 1], past[0:NT, cols], hundred[0:NT, :], start=True, stop=False)
                        last = pe.matmul(shared[:, z:z + 1], earlier[:, cols], one[:], start=False, stop=True)
                    last.then_inc(ids_mm, 1)

            def step(i):
                b, last = i.back(1), i.back(2)
                parity = b.slot(PERIOD) // per
                at = places(i, job)
                if b.live(n) and b.slot(per) == 0:
                    pe.wait_ge(kept, b.use(per, SHARES, SHARES))
                for f in range(nf):
                    ff.gate_up(pe, b, n, f, wg[:, parity], wu[:, parity])
                    at(2 * f)
                    if f == 0:
                        ff.down(pe, last, n, nf - 1, wd[:, last.slot(PERIOD) // per])
                    else:
                        ff.down(pe, b, n, f - 1, wd[:, parity])
                    if f == 3:
                        if i.live(n):
                            pe.wait_ge(got[i.slot(2)], i.use(2, 16 * TILES, 16 * TILES))
                        ff.turn(pe, i, n, lambda t, s: rows[:, t.slot(2), s, 0:PACK // 2].bitcast(F16), k["eye16"])
                    at(2 * f + 1)

            run_steps(pe, n, LEAD, 2, PERIOD, step)


def language_model_block(nc, x, emb, ws, wqkv, w_out, b_out, gate, wg, wu, wd, ws_g, ws_u, ws_d, out):
    NT = x.shape[0]
    T = NT * P
    NB = T // SEQ
    E, F = wg.shape[0], wg.shape[1]
    FS = ws_g.shape[0]
    dims = dict(NT=NT, NB=NB, E=E, F=F, FS=FS, cap=T * 2 // E, group=GROUP)
    stack_dram = nc.dram_tensor("stack", [NB, 2 * HD + 2, HEADS * SEQ], F16).ap()
    v_dram = nc.dram_tensor("values", [NB, P, STEPS, VROW], F32).ap()
    h_dram = nc.dram_tensor("h", [NB, P, STEPS, D], F32).ap()
    h1_dram = nc.dram_tensor("h1", [NB, P, STEPS, D], F32).ap()
    pack_dram = nc.dram_tensor("packs", [T, PACK // 2 + E], U32).ap()
    with Mem(nc, "top") as top:
        k = make_constants(nc, top, ws, x, dims)
        with Mem(nc, "first") as m:
            wqkv_stack = m.sb("wqkv", [P, 4, 2 * D], F16)
            make_stacks(nc, k, "qkv_weights", query_jobs(wqkv, wqkv_stack[:, :, 0:D])
                        + row_jobs(wqkv[D:2 * D, :], D, wqkv_stack[:, :, D:2 * D]))
            embed_and_project(nc, k, dims, emb, b_out, wqkv_stack, stack_dram, v_dram, h_dram)
        mv = top.sb("mv", [P, NT, 2], F32)
        with Mem(nc, "second") as m:
            out_stack = m.sb("w_out", [P, 4, D], F16)
            make_stacks(nc, k, "out_weights", row_jobs(w_out, D, out_stack))
            attention(nc, k, dims, out_stack, mv, stack_dram, v_dram, h_dram, h1_dram)
        with Mem(nc, "rest") as rest:
            counts = rest.sb("counts", [P, E, P], F16)
            before, upto = rest.sb("before", [P, E], F32), rest.sb("upto", [P, E], F32)
            with Mem(nc, "third") as m:
                scores = m.sb("scores", [P, NT, E], F32)
                with Mem(nc, "shared_weights") as weights:
                    w = dict(gate=weights.sb("gate", [P, 4, E], F16), sg=weights.sb("sg", [P, 4, FS], F16),
                             su=weights.sb("su", [P, 4, FS], F16), sd=weights.sb("sd", [P, FS // P, 2, D], F16))
                    make_stacks(nc, k, "gate_weights", row_jobs(gate, E, w["gate"]) + row_jobs(ws_g, FS, w["sg"])
                                + row_jobs(ws_u, FS, w["su"]))
                    make_down(nc, k, "down_weights", ws_d, w["sd"], FS // P)
                    shared_expert(nc, k, dims, w, mv, scores, h1_dram, pack_dram, out)
                choose_tokens(nc, k, dims, scores, counts, before, upto)
            experts(nc, k, dims, counts, before, upto, wg, wu, wd, pack_dram, out)


def kernel(**inputs):
    import numpy as np
    import concourse.bacc as bacc
    from concourse import mybir
    from concourse.bass_utils import run_bass_kernel_spmd

    shapes = {"x": (-1, 128), "L0_tok_weight_scale": (1, 1), "L0_attn_b_out": (1, -1)}
    names = ["x", "L0_tok_weight", "L0_tok_weight_scale", "L0_attn_W_qkv", "L0_attn_W_out", "L0_attn_b_out",
             "L0_ffn_gate_weight", "L0_ffn_Wg", "L0_ffn_Wu", "L0_ffn_Wd", "L0_ffn_Ws_g", "L0_ffn_Ws_u", "L0_ffn_Ws_d"]
    nc = bacc.Bacc("TRN2", target_bir_lowering=False, num_devices=1)
    arrays, args = {}, []
    for name in names:
        a = np.ascontiguousarray(inputs[name])
        if name in shapes:
            a = a.reshape(shapes[name])
        arrays[f"in_{name}"] = a
        args.append(nc.dram_tensor(f"in_{name}", a.shape, mybir.dt.from_np(a.dtype), kind="ExternalInput").ap())
    tokens, d = inputs["x"].shape, inputs["L0_tok_weight"].shape[1]
    out = nc.dram_tensor("out", (tokens[0] * tokens[1], d), mybir.dt.float32, kind="ExternalOutput").ap()
    language_model_block(nc, *args, out)
    r = run_bass_kernel_spmd(nc, [arrays], core_ids=[0])
    return r.results[0]["out"].reshape(tokens[0], tokens[1], d)
```

```python
from contextlib import ExitStack

import concourse.bass as bass
from concourse import mybir

ALU = mybir.AluOpType
ACT = mybir.ActivationFunctionType
AX = mybir.AxisListType
F32 = mybir.dt.float32
F16 = mybir.dt.float16
I32 = mybir.dt.int32
U32 = mybir.dt.uint32

P = 128
D = 192
REST = D - P
HEADS = 12
HD = D // HEADS
SEQ = 256
STEPS = SEQ // P
PACK = 3 * P
SPLIT = 64.0
CHUNKS = ((0, 0), (1, 1), (2, 0), (3, 1), (0, 2))
EPS = 1e-5
QMAX = 127.0
ROUND = 1.5 * 2.0 ** 23
VROW = HEADS * (HD + 1)
GROUP = 4


class At:

    def __init__(self, turn, period, c):
        self.turn, self.period, self.c = turn, period, c

    def back(self, lag):
        return At(self.turn, self.period, self.c - lag)

    def times(self, k, plus=0):
        return self.turn * (self.period * k) + (self.c * k + plus)

    def slot(self, m):
        return self.c % m

    def use(self, m, k=1, plus=0):
        return self.turn * (self.period // m * k) + (self.c // m * k + plus)

    def live(self, n):
        return not isinstance(self.turn, int) or 0 <= self.c < n


def run_steps(eng, n, lead, lag, period, step):
    low = -(-(lag + 3) // period) * period
    high = max((n - lead) // period * period, 0)
    if high - low < 2 * period:
        low = high = n
    for i in range(-lead, low):
        step(At(0, period, i))
    if high > low:
        with eng.Fori(low // period, high // period) as turn:
            for c in range(period):
                step(At(turn, period, c))
    for i in range(high, n + lag):
        step(At(0, period, i))


def need(eng, sem, value, apart=None):
    if not isinstance(value, int) or value > 0:
        eng.wait_ge(sem, value)
        if apart is not None and not isinstance(value, int):
            eng.sem_inc(apart, 1)


class Mem:

    def __init__(self, nc, name):
        self.nc, self.name, self.ctx = nc, name, ExitStack()
        self.used = []

    def __enter__(self):
        self.ctx.__enter__()
        return self

    def __exit__(self, *e):
        done = self.ctx.__exit__(*e)
        if self.used:
            self.nc.clear_and_free_semaphores(self.used)
            self.nc.all_engine_barrier()
        return done

    def sb(self, name, shape, dt):
        return self.ctx.enter_context(self.nc.sbuf_tensor(f"{self.name}_{name}", shape, dt))

    def ps(self, name, shape, dt):
        return self.ctx.enter_context(self.nc.psum_tensor(f"{self.name}_{name}", shape, dt))

    def bank(self, name, dt=F32):
        return self.ps(name, [P, 2048 // (4 if dt == F32 else 2)], dt)

    def sem(self, name):
        self.used.append(self.nc.alloc_semaphore(name=f"{self.name}_{name}"))
        return self.used[-1]

    def sems(self, name, n):
        return [self.sem(f"{name}{i}") for i in range(n)]

    def block(self):
        return self.ctx.enter_context(self.nc.Block())


def make_constants(nc, top, ws_dram, x_dram, dims):
    NT = dims["NT"]
    k = {
        "eye16": top.sb("eye16", [P, P], F16),
        "eye32": top.sb("eye32", [P, P], F32),
        "ws": top.sb("ws", [P, 1], F32),
        "inv_ws": top.sb("inv_ws", [P, 1], F32),
        "eps": top.sb("eps", [P, 1], F32),
        "ids": top.sb("ids", [P, NT], U32),
    }
    with Mem(nc, "const") as m:
        rows = m.sb("rows", [NT, P], I32)
        rowsf = m.sb("rowsf", [NT, P], F32)
        cols = m.bank("cols")[:, 0:NT]
        loaded, zeroed, made = m.sem("loaded"), m.sem("zeroed"), m.sem("made")
        floats, turned, done = m.sem("floats"), m.sem("turned"), m.sem("done")
        block = m.block()

        @block.sync
        def _(sp):
            sp.dma_start(rows[:], x_dram).then_inc(loaded, 16)
            sp.dma_start(k["ws"][:], ws_dram.to_broadcast([P, 1])).then_inc(loaded, 16)

        @block.gpsimd
        def _(pool):
            nc.gpsimd.memset(k["eye16"][:], 0.0).then_inc(zeroed, 1)
            nc.gpsimd.memset(k["eye32"][:], 0.0).then_inc(zeroed, 1)
            pool.wait_ge(zeroed, 2)
            for eye in (k["eye16"], k["eye32"]):
                nc.gpsimd.affine_select(out=eye[:], in_=eye[:], compare_op=ALU.not_equal, fill=1.0, base=0,
                                        pattern=[[-1, P]], channel_multiplier=1).then_inc(made, 1)

        @block.vector
        def _(dve):
            nc.vector.memset(k["eps"][:], EPS)
            dve.wait_ge(loaded, 32)
            nc.vector.tensor_copy(rowsf[:], rows[:]).then_inc(floats, 1)
            nc.vector.reciprocal(k["inv_ws"][:], k["ws"][:])
            dve.wait_ge(turned, 1)
            nc.vector.tensor_copy(k["ids"][:], cols).then_inc(done, 1)

        @block.tensor
        def _(pe):
            pe.wait_ge(made, 2)
            pe.wait_ge(floats, 1)
            pe.transpose(cols, rowsf[:], k["eye32"][0:NT, 0:NT]).then_inc(turned, 1)
    return k


def make_stacks(nc, k, name, jobs):
    tiles = jobs
    with Mem(nc, name) as m:
        LOADS = 4
        nat = m.sb("nat", [P, LOADS, D], F32)
        parts = m.sb("parts", [P, 2, 4 * P], F16)
        turned = [m.bank(f"turned{i}", F16)[:, 0:4 * P].rearrange("p (c n) -> p c n", c=4) for i in range(2)]
        loaded = m.sems("loaded", LOADS)
        hi_done, lo_done, twice, turned_done, kept = (m.sem(x) for x in ("hi", "lo", "twice", "turned_done", "kept"))
        block = m.block()

        @block.sync
        def _(sp):
            for i, (src, n, dst) in enumerate(tiles):
                need(sp, lo_done, i + 1 - LOADS)
                sp.dma_start(nat[0:n, i % LOADS, :], src).then_inc(loaded[i % LOADS], 16)

        @block.scalar
        def _(act):
            for i, (src, n, dst) in enumerate(tiles):
                act.wait_ge(loaded[i % LOADS], 16 * (i // LOADS + 1))
                need(act, turned_done, i - 1)
                nc.scalar.activation(parts[0:n, i % 2, 0:D], nat[0:n, i % LOADS, :], ACT.Copy,
                                     scale=SPLIT).then_inc(hi_done, 1)

        @block.vector
        def _(dve):
            def keep(i):
                src, n, dst = tiles[i]
                dve.wait_ge(turned_done, i + 1)
                columns = turned[i % 2][:, :, 0:n]
                if len(dst.shape) == 4:
                    columns = columns.rearrange("p c (a b) -> p c a b", b=dst.shape[3])
                nc.vector.tensor_copy(dst, columns).then_inc(kept, 1)

            for i, (src, n, dst) in enumerate(tiles):
                dve.wait_ge(hi_done, i + 1)
                nc.vector.scalar_tensor_tensor(out=parts[0:n, i % 2, 2 * P:2 * P + D], in0=nat[0:n, i % LOADS, :],
                                               scalar=SPLIT, in1=parts[0:n, i % 2, 0:D], op0=ALU.mult,
                                               op1=ALU.subtract).then_inc(lo_done, 1)
                if i:
                    keep(i - 1)
            keep(len(tiles) - 1)

        @block.gpsimd
        def _(pool):
            for i, (src, n, dst) in enumerate(tiles):
                pool.wait_ge(lo_done, i + 1)
                for c in (0, 2 * P):
                    last = nc.gpsimd.tensor_copy(parts[0:n, i % 2, c + D:c + 2 * P], parts[0:n, i % 2, c + P:c + D])
                last.then_inc(twice, 1)

        @block.tensor
        def _(pe):
            for i, (src, n, dst) in enumerate(tiles):
                pe.wait_ge(twice, i + 1)
                need(pe, kept, i - 1)
                for c in range(4):
                    last = pe.transpose(turned[i % 2][:, c, 0:n], parts[0:n, i % 2, c * P:(c + 1) * P],
                                        k["eye16"][0:n, 0:n])
                last.then_inc(turned_done, 1)


def row_jobs(src, n, stack):
    return [(src[r:min(r + P, n), :], min(P, n - r), stack[:, :, r:min(r + P, n)]) for r in range(0, n, P)]


def query_jobs(src, stack):
    by_head = stack.rearrange("p c (d h) -> p c h d", h=HEADS)
    heads = P // HD
    return [(src[r:min(r + P, D), :], min(P, D - r), by_head[:, :, r // HD:min(r // HD + heads, HEADS), :])
            for r in range(0, D, P)]


def embed_and_project(nc, k, dims, emb, wqkv, stack_dram, v_dram, h_dram):
    NB = dims["NB"]
    with Mem(nc, "emb") as m:
        picked = m.sb("picked", [P, 2, STEPS], U32)
        picked_done, apart = m.sem("picked_done"), m.sem("apart")
        row = m.sb("row", [P, 2, STEPS, D], F32)
        q = m.sb("q", [P, 2, STEPS, D], F32)
        h0 = m.sb("h0", [P, 2, STEPS, D], F32)
        stats = m.sb("stats", [P, 2, STEPS, 6], F32)
        mv = m.sb("mv", [P, 2, STEPS, 2], F32)
        std = m.sb("std", [P, 2, STEPS], F32)
        rstd = m.sb("rstd", [P, 2, STEPS], F32)
        xn = m.sb("xn", [P, 2, STEPS, D], F32)
        pack = m.sb("pack", [P, 2, STEPS, PACK], F16)
        chunks = m.sb("chunks", [P, 2, 3, SEQ], F16)
        wide_picks = m.sb("wide_picks", [P, 2, HEADS, HD], F32)
        picks = m.sb("picks", [P, 2, HEADS], F32)
        q_parts = m.sb("q_parts", [P, 2, 2, 2, SEQ], F16)
        q_sq = m.sb("q_sq", [P, 2, SEQ], F32)
        s_parts = m.sb("s_parts", [HEADS, 2, 2, SEQ], F16)
        vals = m.sb("vals", [P, 2, STEPS, VROW], F32)
        chunk_bank = m.bank("chunk_ps", F16)
        chunk_ps = chunk_bank[:].rearrange("p (c n) -> p c n", n=SEQ)
        q_ps = [m.bank(f"q_ps{i}")[:].rearrange("p (c n) -> p c n", n=SEQ) for i in range(2)]
        v_ps = [m.bank(f"v_ps{i}")[:, 0:STEPS * D].rearrange("p (s d) -> p s d", d=D) for i in range(2)]
        s_ps = [m.bank(f"s_ps{i}")[0:HEADS, 0:SEQ] for i in range(2)]
        (quarters, set_up, h0_done, scaled, clipped, stat_done, aggr_done, std_done, rstd_done,
         xn_done, hi_done, lo_done, turned, chunks_done, q_mm, v_mm, qhi_done, qlo_done, qsq_done, v_done,
         s_mm, shi_done, slo_done) = (m.sem(x) for x in (
             "quarters", "set_up", "h0_done", "scaled", "clipped", "stat_done", "aggr_done",
             "std_done", "rstd_done", "xn_done", "hi_done", "lo_done", "turned", "chunks_done", "q_mm",
             "v_mm", "qhi_done", "qlo_done", "qsq_done", "v_done", "s_mm", "shi_done", "slo_done"))
        got = m.sems("got", 2)
        h_out, v_out, stack_out = m.sems("h_out", 2), m.sems("v_out", 2), m.sems("stack_out", 2)
        inv = 1.0 / SPLIT
        squares_out = m.sems("squares_out", 2)
        WRITES = 2
        block = m.block()

        @block.gpsimd
        def _(pool):
            nc.gpsimd.memset(wide_picks[:], 0.0).then_inc(quarters, 1)
            pool.wait_ge(quarters, 1)
            for half in range(2):
                nc.gpsimd.affine_select(out=wide_picks[:, half], in_=wide_picks[:, half], compare_op=ALU.not_equal,
                                        fill=-0.5, base=P * half, pattern=[[-1, HEADS], [-HEADS, HD]],
                                        channel_multiplier=1).then_inc(quarters, 1)

            def step(i):
                t = i.back(-1)
                if t.live(NB):
                    a = t.slot(2)
                    need(pool, scaled, t.times(1, -1))
                    nc.gpsimd.tensor_copy(picked[:, a, :], ids_of(t)).then_inc(picked_done, 1)
                    need(pool, picked_done, t.times(1, 1), apart)
                    for s in range(STEPS):
                        nc.gpsimd.indirect_dma_start(
                            out=row[:, a, s, :], out_offset=None, in_=emb,
                            in_offset=bass.IndirectOffsetOnAxis(ap=picked[:, a, s:s + 1], axis=0)).then_inc(got[a], 16)
                t = i.back(1)
                if t.live(NB):
                    a = t.slot(2)
                    pool.wait_ge(hi_done, t.times(1, 1))
                    nc.gpsimd.tensor_tensor(pack[:, a, :, D:2 * P], xn[:, a, :, P:D], pack[:, a, :, P:D], ALU.subtract)
                    nc.gpsimd.tensor_tensor(pack[:, a, :, 2 * P:PACK], xn[:, a, :, 0:P], pack[:, a, :, 0:P],
                                            ALU.subtract).then_inc(lo_done, 1)

            def ids_of(t):
                if isinstance(t.turn, int):
                    return k["ids"][:, STEPS * t.c:STEPS * t.c + STEPS]
                return k["ids"][:, bass.ds(t.times(STEPS), STEPS)]

            run_steps(pool, NB, 1, 1, 2, step)

        @block.vector
        def _(dve):
            for a in range(2):
                nc.vector.memset(vals[:, a], 1.0)
            nc.vector.memset(chunk_bank[:].bitcast(F32), 0.0).then_inc(set_up, 1)
            dve.wait_ge(quarters, 3)
            nc.vector.tensor_reduce(picks[:], wide_picks[:], AX.X, ALU.add).then_inc(set_up, 1)


            def scaled_rows(i):
                if i.live(NB):
                    a = i.slot(2)
                    dve.wait_ge(got[a], i.use(2, 16 * STEPS, 16 * STEPS))
                    nc.vector.tensor_scalar(q[:, a], row[:, a], k["inv_ws"][:], QMAX, ALU.mult, ALU.min).then_inc(scaled, 1)

            def rounded_rows(i):
                if i.live(NB):
                    a = i.slot(2)
                    dve.wait_ge(scaled, i.times(1, 1))
                    nc.vector.tensor_scalar(q[:, a], q[:, a], -QMAX, ROUND, ALU.max, ALU.add).then_inc(clipped, 1)

            def quantised_rows(i):
                if i.live(NB):
                    a = i.slot(2)
                    need(dve, xn_done, i.times(1, -1))
                    need(dve, h_out[a], i.use(2, 16))
                    dve.wait_ge(clipped, i.times(1, 1))
                    nc.vector.tensor_scalar(h0[:, a], q[:, a], -ROUND, k["ws"][:], ALU.add, ALU.mult).then_inc(h0_done, 1)

            def statistics(i):
                if i.live(NB):
                    dve.wait_ge(h0_done, i.times(1, 1))
                    for s in range(STEPS):
                        last = nc.vector.bn_stats(stats[:, i.slot(2), s, :], h0[:, i.slot(2), s, :])
                    last.then_inc(stat_done, 1)

            def moments(i):
                if i.live(NB):
                    need(dve, stat_done, i.times(1, 1), apart)
                    for s in range(STEPS):
                        last = nc.vector.bn_aggr(mv[:, i.slot(2), s, :], stats[:, i.slot(2), s, :])
                    last.then_inc(aggr_done, 1)

            def inverse_deviations(t):
                if t.live(NB):
                    dve.wait_ge(std_done, t.times(1, 1))
                    nc.vector.reciprocal(rstd[:, t.slot(2)], std[:, t.slot(2)]).then_inc(rstd_done, 1)

            def normalised_rows(t):
                if t.live(NB):
                    a = t.slot(2)
                    dve.wait_ge(rstd_done, t.times(1, 1))
                    need(dve, lo_done, t.times(1, -1))
                    for s in range(STEPS):
                        last = nc.vector.tensor_scalar(xn[:, a, s, :], h0[:, a, s, :], mv[:, a, s, 0:1], rstd[:, a, s:s + 1],
                                                       ALU.subtract, ALU.mult)
                    last.then_inc(xn_done, 1)

            def query_rest(t, half):
                if t.live(NB):
                    a, rows = t.slot(2), (P, REST)[half]
                    if half == 0:
                        dve.wait_ge(qhi_done, t.times(1, 1))
                        need(dve, stack_out[a], t.use(2, 16 * WRITES))
                    nc.vector.scalar_tensor_tensor(
                        out=q_parts[0:rows, a, 1, half, :], in0=q_ps[a][0:rows, half, :], scalar=inv,
                        in1=q_parts[0:rows, a, 0, half, :], op0=ALU.mult, op1=ALU.subtract).then_inc(qlo_done, 1)

            def square_rest(t):
                if t.live(NB):
                    dve.wait_ge(shi_done, t.times(1, 1))
                    need(dve, squares_out[t.slot(2)], t.use(2, 16))
                    nc.vector.tensor_tensor(s_parts[:, t.slot(2), 1, :], s_ps[t.slot(2)], s_parts[:, t.slot(2), 0, :],
                                            ALU.subtract).then_inc(slo_done, 1)

            def step(i):
                scaled_rows(i)
                inverse_deviations(i.back(1))
                rounded_rows(i)
                normalised_rows(i.back(1))
                quantised_rows(i)
                statistics(i)
                query_rest(i.back(4), 0)
                moments(i)
                query_rest(i.back(4), 1)
                square_rest(i.back(5))

            run_steps(dve, NB, 0, 5, 2, step)

        @block.scalar
        def _(act):
            act.wait_ge(set_up, 1)

            def deviations(t):
                if t.live(NB):
                    a = t.slot(2)
                    act.wait_ge(aggr_done, t.times(1, 1))
                    need(act, rstd_done, t.times(1, -1))
                    nc.scalar.activation(std[:, a], mv[:, a, :, 1], ACT.Sqrt, bias=k["eps"][:]).then_inc(std_done, 1)

            def keep_queries(t):
                if t.live(NB):
                    a = t.slot(2)
                    act.wait_ge(q_mm, t.times(1, 1))
                    need(act, s_mm, t.times(1, 0))
                    nc.scalar.activation(q_sq[:, 0, :], q_ps[a][:, 0, :], ACT.Square, scale=inv)
                    nc.scalar.activation(q_sq[0:REST, 1, :], q_ps[a][0:REST, 1, :], ACT.Square,
                                         scale=inv).then_inc(qsq_done, 1)
                    need(act, stack_out[a], t.use(2, 16 * WRITES))
                    for half, n in ((0, P), (1, REST)):
                        last = nc.scalar.activation(q_parts[0:n, a, 0, half, :], q_ps[a][0:n, half, :], ACT.Copy, scale=inv)
                    last.then_inc(qhi_done, 1)

            def keep_values(t):
                if t.live(NB):
                    a = t.slot(2)
                    act.wait_ge(v_mm, t.times(1, 1))
                    need(act, v_out[a], t.use(2, 16))
                    nc.scalar.activation(
                        vals[:, a].rearrange("p s (h d) -> p (s h) d", d=HD + 1)[:, :, 0:HD],
                        v_ps[a].rearrange("p s (h d) -> p (s h) d", d=HD), ACT.Copy, scale=inv).then_inc(v_done, 1)

            def keep_chunks(t):
                if t.live(NB):
                    a = t.slot(2)
                    act.wait_ge(turned, t.times(1, 1))
                    need(act, v_mm, t.times(1, -1))
                    nc.scalar.copy(chunks[:, a], chunk_ps[:, 0:3]).then_inc(chunks_done, 1)

            def split(t):
                if t.live(NB):
                    a = t.slot(2)
                    act.wait_ge(xn_done, t.times(1, 1))
                    need(act, turned, t.times(1, -1))
                    nc.scalar.copy(pack[:, a, :, 0:D], xn[:, a]).then_inc(hi_done, 1)

            def keep_squares(t):
                if t.live(NB):
                    a = t.slot(2)
                    act.wait_ge(s_mm, t.times(1, 1))
                    need(act, squares_out[a], t.use(2, 16))
                    nc.scalar.copy(s_parts[:, a, 0, :], s_ps[a]).then_inc(shi_done, 1)

            def step(i):
                deviations(i.back(1))
                keep_queries(i.back(4))
                keep_values(i.back(4))
                split(i.back(1))
                keep_chunks(i.back(2))
                keep_squares(i.back(5))

            run_steps(act, NB, 0, 5, 2, step)

        @block.tensor
        def _(pe):
            pe.wait_ge(set_up, 2)

            def step(i):
                t = i.back(2)
                if t.live(NB):
                    a = t.slot(2)
                    pe.wait_ge(lo_done, t.times(1, 1))
                    need(pe, chunks_done, t.times(1, 0))
                    for s in range(STEPS):
                        for c in range(3):
                            last = pe.transpose(chunk_ps[:, c, s * P:(s + 1) * P], pack[:, a, s, c * P:(c + 1) * P], k["eye16"][:])
                    last.then_inc(turned, 1)
                t = i.back(3)
                if t.live(NB):
                    a = t.slot(2)
                    pe.wait_ge(chunks_done, t.times(1, 1))
                    need(pe, qlo_done, t.times(2, -2))
                    for half, n in ((0, P), (1, REST)):
                        for c, (w, x) in enumerate(CHUNKS):
                            last = pe.matmul(q_ps[a][0:n, half, :], wqkv[:, w, half * P:half * P + n], chunks[:, a, x, :],
                                             start=c == 0, stop=c == len(CHUNKS) - 1)
                    last.then_inc(q_mm, 1)
                    need(pe, v_done, t.times(1, -1))
                    for s in range(STEPS):
                        for c, (w, x) in enumerate(CHUNKS):
                            last = pe.matmul(v_ps[a][:, s, :], chunks[:, a, x, s * P:(s + 1) * P], wqkv[:, w, D:2 * D],
                                             start=c == 0, stop=c == len(CHUNKS) - 1)
                    last.then_inc(v_mm, 1)
                t = i.back(4)
                if t.live(NB):
                    a = t.slot(2)
                    pe.wait_ge(qsq_done, t.times(1, 1))
                    need(pe, slo_done, t.times(1, -1))
                    pe.matmul(s_ps[a], picks[:, 0, :], q_sq[:, 0, :], start=True, stop=False)
                    pe.matmul(s_ps[a], picks[0:REST, 1, :], q_sq[0:REST, 1, :], start=False, stop=True).then_inc(s_mm, 1)

            run_steps(pe, NB, 0, 5, 2, step)

        @block.sync
        def _(sp):
            def step(i):
                if i.live(NB):
                    sp.wait_ge(h0_done, i.times(1, 1))
                    sp.dma_start(h_dram[seq_of(i)], h0[:, i.slot(2)]).then_inc(h_out[i.slot(2)], 16)
                t = i.back(4)
                if t.live(NB):
                    a = t.slot(2)
                    sp.wait_ge(v_done, t.times(1, 1))
                    sp.dma_start(v_dram[seq_of(t)], vals[:, a]).then_inc(v_out[a], 16)
                if t.live(NB):
                    sp.wait_ge(qlo_done, t.times(2, 2))
                    rows = stack_dram[seq_of(t)][0:2 * HD, :].rearrange("(c d) (h n) -> (d h) c n", c=2, h=HEADS)
                    for half, n in ((0, P), (1, REST)):
                        sp.dma_start(rows[half * P:half * P + n], q_parts[0:n, a, :, half, :]).then_inc(stack_out[a], 16)
                t = i.back(5)
                if t.live(NB):
                    a = t.slot(2)
                    sp.wait_ge(slo_done, t.times(1, 1))
                    sp.dma_start(stack_dram[seq_of(t)][2 * HD:2 * HD + 2, :].rearrange("c (h n) -> h c n", h=HEADS),
                                 s_parts[:, a]).then_inc(squares_out[a], 16)

            def seq_of(t):
                return t.c if isinstance(t.turn, int) else t.times(1)

            run_steps(sp, NB, 0, 5, 2, step)
            for a in range(2):
                uses = (NB - a + 1) // 2
                sp.wait_ge(h_out[a], 16 * uses)
                sp.wait_ge(v_out[a], 16 * uses)
                sp.wait_ge(stack_out[a], 16 * WRITES * uses)
                sp.wait_ge(squares_out[a], 16 * uses)


def attention(nc, k, dims, w_out, b_out, mv, stack_dram, v_dram, h_dram, h1_dram):
    NB, group = dims["NB"], dims["group"]
    R = 2 * group
    lag, out, turned_at, post = R - 1, R, R + 1, R + 2
    inv = 1.0 / SPLIT
    W = 3 * P
    with Mem(nc, "att") as m:
        moving = m.sb("moving", [P, 2, HEADS, SEQ], F16)
        fixed = m.sb("fixed", [P, 2, HEADS, SEQ], F16)
        dist = [m.sb(f"dist{i}", [P, HEADS, W], F32) for i in range(R)]
        vals = m.sb("vals", [P, 2, STEPS * VROW + 2 * HD], F32)
        e10 = m.sb("e10", [P, 2, 4, P], F32)
        o_sb = m.sb("o_sb", [P, 3, SEQ], F32)
        recip = m.sb("recip", [P, STEPS, HEADS], F32)
        att = m.sb("att", [P, STEPS, D], F32)
        pack = m.sb("pack", [P, STEPS, PACK], F16)
        chunks = m.sb("chunks", [P, 3, SEQ], F16)
        hb = m.sb("hb", [P, 2, STEPS, D], F32)
        h1 = m.sb("h1", [P, 2, STEPS, D], F32)
        stats = m.sb("stats", [P, STEPS, 6], F32)
        bias = m.sb("bias", [P, D], F32)
        bias_parts = m.sb("bias_parts", [P, 2, D], F16)
        share = m.sb("share", [P, P], F16)
        d_ps = [m.bank(f"d_ps{i}") for i in range(3)]
        t_ps = m.bank("t_ps")[:].rearrange("p (h n) -> p h n", n=P)
        o_ps = m.ps("o_ps", [P, 4, SEQ], F32)
        x_ps = m.bank("x_ps")
        c_ps = m.bank("c_ps", F16)[:].rearrange("p (c n) -> p c n", n=SEQ)
        (dist_mm, clamped, rooted, exped, turned, e10_done, pv_done, o_done, ot_done, recip_done, att_done,
         hi_done, lo_done, xt_done, chunks_done, wo_done, h1_done, stat_done, aggr_done, apart) = (m.sem(x) for x in (
             "dist_mm", "clamped", "rooted", "exped", "turned", "e10_done", "pv_done", "o_done", "ot_done",
             "recip_done", "att_done", "hi_done", "lo_done", "xt_done", "chunks_done", "wo_done", "h1_done",
             "stat_done", "aggr_done", "apart"))
        padded, set_up = m.sem("padded"), m.sems("set_up", 2)
        bias_in, bias_hi, bias_lo = m.sem("bias_in"), m.sem("bias_hi"), m.sem("bias_lo")
        stack_in, v_in, hb_in, h1_out = (m.sems(x, 2) for x in ("stack_in", "v_in", "hb_in", "h1_out"))
        LOADS = 8
        block = m.block()

        def at(dram, t):
            return dram[t.c if isinstance(t.turn, int) else t.times(1)]

        def fixed_rows(engine, waits, a):
            for stack in (moving, fixed):
                engine.memset(stack[64:P, a].bitcast(F32), 0.0).then_inc(set_up[a], 1)
            waits.wait_ge(set_up[a], 2)
            for stack in (moving, fixed):
                engine.memset(stack[64:68, a], 1.0).then_inc(set_up[a], 1)

        @block.gpsimd
        def _(pool):
            fixed_rows(nc.gpsimd, pool, 1)

            def step(i):
                t = i.back(turned_at)
                if t.live(NB):
                    need(pool, att_done, t.times(2, 2), apart)
                    need(pool, xt_done, t.times(1, 0), apart)
                    nc.gpsimd.tensor_copy(pack[:, :, 0:D], att[:]).then_inc(hi_done, 1)
                    pool.wait_ge(hi_done, t.times(1, 1))
                    nc.gpsimd.tensor_tensor(pack[:, :, D:2 * P], att[:, :, P:D], pack[:, :, P:D], ALU.subtract)
                    nc.gpsimd.tensor_tensor(pack[:, :, 2 * P:PACK], att[:, :, 0:P], pack[:, :, 0:P],
                                            ALU.subtract).then_inc(lo_done, 1)

            run_steps(pool, NB, 0, post, R, step)

        @block.sync
        def _(sp):
            def load(t):
                a = t.slot(2)
                if isinstance(t.turn, int) and t.c == 0:
                    sp.dma_start(bias[:], b_out.to_broadcast([P, D])).then_inc(bias_in, 16)
                if isinstance(t.turn, int) and t.c < 2:
                    sp.wait_ge(set_up[t.c], 4)
                need(sp, dist_mm, t.times(HEADS, -HEADS))
                rows = at(stack_dram, t)
                two = rows[0:2 * HD, :]
                def flat(x):
                    return x.rearrange("p h n -> p (h n)")
                sp.dma_start(flat(moving[0:2 * HD, a]), two).then_inc(stack_in[a], 16)
                sp.dma_start(flat(moving[2 * HD:4 * HD, a]), two).then_inc(stack_in[a], 16)
                sp.dma_start(flat(moving[64:66, a]), rows[2 * HD:2 * HD + 2, :]).then_inc(stack_in[a], 16)
                for part in range(2):
                    for copy in range(2):
                        at_row = (2 * part + copy) * HD
                        sp.dma_start(flat(fixed[at_row:at_row + HD, a]),
                                     rows[part * HD:(part + 1) * HD, :]).then_inc(stack_in[a], 16)
                sp.dma_start(flat(fixed[66:68, a]), rows[2 * HD:2 * HD + 2, :]).then_inc(stack_in[a], 16)

            def step(i):
                t = i.back(-1)
                if t.live(NB):
                    load(t)
                t = i.back(lag - 1)
                if t.live(NB):
                    a = t.slot(2)
                    if isinstance(t.turn, int) and t.c == 0:
                        sp.wait_ge(padded, 1)
                    need(sp, pv_done, t.times(3, -3))
                    sp.dma_start(vals[:, a, 0:STEPS * VROW].rearrange("p (s r) -> p s r", s=STEPS),
                                 at(v_dram, t)).then_inc(v_in[a], 16)
                t = i.back(post - 1)
                if t.live(NB):
                    a = t.slot(2)
                    need(sp, h1_done, t.times(1, -1))
                    sp.dma_start(hb[:, a], at(h_dram, t)).then_inc(hb_in[a], 16)
                t = i.back(post)
                if t.live(NB):
                    a = t.slot(2)
                    sp.wait_ge(h1_done, t.times(1, 1))
                    sp.dma_start(at(h1_dram, t), h1[:, a]).then_inc(h1_out[a], 16)

            run_steps(sp, NB, 1, post, R, step)
            for a in range(2):
                sp.wait_ge(h1_out[a], 16 * ((NB - a + 1) // 2))


        @block.tensor
        def _(pe):
            def distances(i, heads):
                if not i.live(NB):
                    return
                a = i.slot(2)
                for h in heads:
                    if h == 0:
                        pe.wait_ge(stack_in[a], i.use(2, 16 * LOADS, 16 * LOADS))
                    need(pe, clamped, i.times(HEADS, h - 2))
                    pe.matmul(d_ps[h % 3][:, 0:SEQ], fixed[:, a, h, 0:P], moving[:, a, h, :], start=True, stop=True)
                    pe.matmul(d_ps[h % 3][:, SEQ:W], fixed[:, a, h, P:SEQ], moving[:, a, h, P:SEQ],
                              start=True, stop=True).then_inc(dist_mm, 1)

            def turn(v, g):
                if v.live(NB):
                    if g == 0:
                        pe.wait_ge(exped, v.times(1, 1))
                    need(pe, e10_done, v.times(3, g))
                    for h in range(4):
                        last = pe.transpose(t_ps[:, h, :], dist[v.slot(R)][:, 4 * g + h, P:SEQ], k["eye32"][:])
                    last.then_inc(turned, 1)

            def values(v, g):
                if not v.live(NB):
                    return
                a = v.slot(2)
                if g == 0:
                    pe.wait_ge(v_in[a], v.use(2, 16, 16))
                    need(pe, o_done, v.times(1, 0))
                e = dist[v.slot(R)]
                pe.wait_ge(e10_done, v.times(3, g + 1))
                for h in range(4):
                    q, col = slice(32 * h, 32 * h + 32), (4 * g + h) * (HD + 1)
                    pe.matmul(o_ps[q, g, :], vals[:, a, col:col + 32], e[:, 4 * g + h, 0:SEQ],
                              start=True, stop=False, skip_group_check=True)
                for h in range(4):
                    q, col = slice(32 * h, 32 * h + 32), VROW + (4 * g + h) * (HD + 1)
                    pe.matmul(o_ps[q, g, 0:P], vals[:, a, col:col + 32], e10[:, (v.slot(2) + g) % 2, h, :],
                              start=False, stop=True, skip_group_check=True)
                for h in range(4):
                    q, col = slice(32 * h, 32 * h + 32), VROW + (4 * g + h) * (HD + 1)
                    last = pe.matmul(o_ps[q, g, P:SEQ], vals[:, a, col:col + 32], e[:, 4 * g + h, SEQ:W],
                                     start=False, stop=True, skip_group_check=True)
                last.then_inc(pv_done, 1)

            def turn_out(r, s):
                if r.live(NB):
                    if s == 0:
                        pe.wait_ge(o_done, r.times(1, 1))
                        need(pe, h1_done, r.times(1, -1))
                    else:
                        pe.wait_ge(att_done, r.times(2, 1))
                    for g in range(3):
                        last = pe.transpose(x_ps[:, g * P:(g + 1) * P], o_sb[:, g, s * P:(s + 1) * P], k["eye32"][:])
                    last.then_inc(ot_done, 1)

            def turn_pack(r):
                if r.live(NB):
                    pe.wait_ge(lo_done, r.times(1, 1))
                    need(pe, chunks_done, r.times(1, 0))
                    for s in range(STEPS):
                        for c in range(3):
                            last = pe.transpose(c_ps[:, c, s * P:(s + 1) * P], pack[:, s, c * P:(c + 1) * P], k["eye16"][:])
                    last.then_inc(xt_done, 1)

            def project(r):
                if r.live(NB):
                    pe.wait_ge(chunks_done, r.times(1, 1))
                    if isinstance(r.turn, int) and r.c == NB - 1:
                        pe.wait_ge(h1_done, NB - 1)
                    else:
                        pe.wait_ge(att_done, r.times(2, 4))
                    for s in range(STEPS):
                        for c, (w, x) in enumerate(CHUNKS):
                            pe.matmul(x_ps[:, s * D:(s + 1) * D], chunks[:, x, s * P:(s + 1) * P], w_out[:, w, :],
                                      start=c == 0, stop=False)
                        for part in range(2):
                            last = pe.matmul(x_ps[:, s * D:(s + 1) * D], share[:], bias_parts[:, part, :],
                                             start=False, stop=part == 1)
                    last.then_inc(wo_done, 1)

            def step(i):
                v, r = i.back(lag), i.back(turned_at)
                distances(i, (0, 1))
                turn_out(r, 0)
                distances(i, (2, 3, 4))
                turn_out(r, 1)
                distances(i, (5, 6))
                turn(v, 0)
                distances(i, (7,))
                project(i.back(post))
                distances(i, (8,))
                turn(v, 1)
                values(v, 0)
                distances(i, (9,))
                turn_pack(r)
                turn(v, 2)
                values(v, 1)
                distances(i, (10, 11))
                values(v, 2)

            pe.wait_ge(bias_lo, 2)
            run_steps(pe, NB, 0, post, R, step)

        @block.vector
        def _(dve):
            nc.vector.memset(vals[:, :, STEPS * VROW:], 0.0).then_inc(padded, 1)
            fixed_rows(nc.vector, dve, 0)
            nc.vector.memset(share[:], 1.0 / P).then_inc(bias_lo, 1)
            dve.wait_ge(bias_hi, 1)
            nc.vector.scalar_tensor_tensor(out=bias_parts[:, 1], in0=bias[:], scalar=SPLIT, in1=bias_parts[:, 0],
                                           op0=ALU.mult, op1=ALU.subtract).then_inc(bias_lo, 1)

            def clamp(i, heads):
                if not i.live(NB):
                    return
                for h in heads:
                    dve.wait_ge(dist_mm, i.times(HEADS, h + 1))
                    if h == 0:
                        need(dve, pv_done, i.times(3, 3 - 3 * R))
                    nc.vector.tensor_scalar(dist[i.slot(R)][:, h, :], d_ps[h % 3][:, 0:W], 0.0, None,
                                            ALU.min).then_inc(clamped, 1)

            def keep_turned(v, g):
                if v.live(NB):
                    dve.wait_ge(turned, v.times(3, g + 1))
                    need(dve, pv_done, v.times(3, g - 1))
                    nc.vector.tensor_copy(e10[:, (v.slot(2) + g) % 2], t_ps).then_inc(e10_done, 1)

            def normalise(r, s):
                if r.live(NB):
                    dve.wait_ge(ot_done, r.times(2, s + 1))
                    heads = x_ps[:, 0:W].rearrange("p (h d) -> p h d", d=32)
                    nc.vector.reciprocal(recip[:, s, :], heads[:, :, HD]).then_inc(recip_done, 1)
                    dve.wait_ge(recip_done, r.times(2, s + 1))
                    if s == 0:
                        need(dve, lo_done, r.times(1, 0))
                    nc.vector.tensor_tensor(att[:, s, :].rearrange("p (h d) -> p h d", d=HD), heads[:, :, 0:HD],
                                            recip[:, s, :, None].to_broadcast([P, HEADS, HD]),
                                            ALU.mult).then_inc(att_done, 1)

            def add_rows(r):
                if r.live(NB):
                    a = r.slot(2)
                    dve.wait_ge(wo_done, r.times(1, 1))
                    dve.wait_ge(hb_in[a], r.use(2, 16, 16))
                    need(dve, h1_out[a], r.use(2, 16, 0))
                    nc.vector.scalar_tensor_tensor(out=h1[:, a], in0=x_ps[:, 0:STEPS * D].rearrange("p (s d) -> p s d", d=D),
                                                   scalar=inv, in1=hb[:, a], op0=ALU.mult, op1=ALU.add).then_inc(h1_done, 1)
                    dve.wait_ge(h1_done, r.times(1, 1))
                    need(dve, aggr_done, r.times(1, 0))
                    for s in range(STEPS):
                        last = nc.vector.bn_stats(stats[:, s, :], h1[:, a, s, :])
                    last.then_inc(stat_done, 1)

            def aggregate(r):
                if r.live(NB):
                    need(dve, stat_done, r.times(1, 1), apart)
                    for s in range(STEPS):
                        last = nc.vector.bn_aggr(moments[:, s, :], stats[:, s, :])
                    last.then_inc(aggr_done, 1)

            def keep_moments(r):
                if r.live(NB):
                    dve.wait_ge(aggr_done, r.times(1, 1))
                    into = mv[:, STEPS * r.c:STEPS * r.c + STEPS, :] if isinstance(r.turn, int) else \
                        mv[:, bass.ds(r.times(STEPS), STEPS), :]
                    nc.vector.tensor_copy(into, moments[:])

            def step(i):
                v, r, last = i.back(lag), i.back(turned_at), i.back(post)
                clamp(i, (0, 1))
                normalise(r, 0)
                clamp(i, (2, 3, 4))
                normalise(r, 1)
                clamp(i, (5, 6))
                keep_turned(v, 0)
                clamp(i, (7, 8))
                keep_turned(v, 1)
                add_rows(last)
                clamp(i, (9,))
                keep_turned(v, 2)
                clamp(i, (10,))
                aggregate(last)
                clamp(i, (11,))
                keep_moments(last)

            moments = m.sb("moments", [P, STEPS, 2], F32)
            run_steps(dve, NB, 0, post, R, step)

        @block.scalar
        def _(act):
            act.wait_ge(bias_in, 16)
            nc.scalar.activation(bias_parts[:, 0], bias[:], ACT.Copy, scale=SPLIT).then_inc(bias_hi, 1)

            def bulk(i, n):
                phase = i.slot(R)
                first = i.back(phase % group)
                t = first.back(group - 2 * (phase % (group // 2)) - n)
                if not t.live(NB):
                    return
                whole = dist[t.slot(R)][:]
                if phase % group < group // 2:
                    act.wait_ge(clamped, t.times(HEADS, HEADS))
                    nc.scalar.activation(whole, whole, ACT.Sqrt, scale=-2.0).then_inc(rooted, 1)
                else:
                    act.wait_ge(rooted, t.times(1, 1))
                    nc.scalar.activation(whole, whole, ACT.Exp, scale=-float(HD) ** -0.5).then_inc(exped, 1)

            def keep_chunks(r):
                if r.live(NB):
                    act.wait_ge(xt_done, r.times(1, 1))
                    need(act, wo_done, r.times(1, 0))
                    nc.scalar.copy(chunks[:], c_ps[:, 0:3, :]).then_inc(chunks_done, 1)

            def keep_out(v):
                if v.live(NB):
                    act.wait_ge(pv_done, v.times(3, 3))
                    need(act, ot_done, v.times(2, 0))
                    nc.scalar.copy(o_sb[:], o_ps[:, 0:3, :]).then_inc(o_done, 1)

            def step(i):
                bulk(i, 0)
                keep_chunks(i.back(post))
                keep_out(i.back(out))
                bulk(i, 1)

            run_steps(act, NB, 0, post, R, step)


TILES = 4
BLOCK = TILES * P


class FeedForward:

    def __init__(self, nc, m, nf, y_done, turns=True):
        self.nc, self.nf, self.y_done = nc, nf, y_done
        self.silu = m.sb("silu", [P, 2, BLOCK], F32)
        self.h_hi = m.sb("h_hi", [P, 3, BLOCK], F16)
        self.h_lo = m.sb("h_lo", [P, 3, BLOCK], F16)
        if turns:
            self.chunks = m.sb("chunks", [P, 2, 3, BLOCK], F16)
            self.c_ps = m.ps("c_ps", [P, 4, BLOCK], F16)
        self.g_ps, self.u_ps, self.h_ps = m.bank("g_ps"), m.bank("u_ps"), m.bank("h_ps")
        self.y_ps = m.ps("y_ps", [P, 2, 512], F32)
        (self.turned, self.chunks_done, self.g_mm, self.u_mm, self.silu_done, self.h_done, self.hi_done,
         self.lo_done, self.down_mm) = (m.sem(x) for x in (
             "turned", "chunks_done", "g_mm", "u_mm", "silu_done", "h_done", "hi_done", "lo_done", "down_mm"))

    def y_tile(self, t):
        return self.y_ps[:, t // 2, t % 2 * D:(t % 2 + 1) * D]

    def turn(self, pe, b, n, rows, eye):
        if b.live(n):
            need(pe, self.chunks_done, b.times(1, 0))
            for t in range(TILES):
                for c in range(3):
                    last = pe.transpose(self.c_ps[:, c, t * P:(t + 1) * P], rows(b, t)[:, c * P:(c + 1) * P], eye[:])
            last.then_inc(self.turned, 1)

    def gate_up(self, pe, b, n, f, wg, wu, chunks):
        if not b.live(n):
            return
        nf = self.nf
        need(pe, self.silu_done, b.times(nf, f))
        for ps, w, done in ((self.g_ps, wg, self.g_mm), (self.u_ps, wu, self.u_mm)):
            if ps is self.u_ps:
                need(pe, self.h_done, b.times(nf, f))
            for c, (s, x) in enumerate(CHUNKS):
                last = pe.matmul(ps[:], w[:, s, f * P:(f + 1) * P], chunks[:, x, :],
                                 start=c == 0, stop=c == len(CHUNKS) - 1)
            last.then_inc(done, 1)

    def down(self, pe, b, n, f, wd):
        if not b.live(n):
            return
        pe.wait_ge(self.lo_done, b.times(self.nf, f + 1))
        if f == 0:
            need(pe, self.y_done, b.times(1, 0))
        for t in range(TILES):
            cols = slice(t * P, (t + 1) * P)
            for c, (h, part) in enumerate(((self.h_hi, 0), (self.h_hi, 1), (self.h_lo, 0))):
                last = pe.matmul(self.y_tile(t), h[:, f % 3, cols], wd[:, f, part, :],
                                 start=f == 0 and c == 0 and t % 2 == 0, stop=f == self.nf - 1 and c == 2,
                                 skip_group_check=True)
        last.then_inc(self.down_mm, 1)

    def keep_chunks(self, act, b, n):
        if b.live(n):
            act.wait_ge(self.turned, b.times(1, 1))
            need(act, self.u_mm, b.times(self.nf, -self.nf))
            self.nc.scalar.copy(self.chunks[:, b.slot(2)], self.c_ps[:, 0:3, :]).then_inc(self.chunks_done, 1)

    def activate(self, act, b, n, f):
        if not b.live(n):
            return
        nf, s = self.nf, (b.slot(2) * self.nf + f) % 2
        act.wait_ge(self.g_mm, b.times(nf, f + 1))
        need(act, self.h_done, b.times(nf, f - 1))
        self.nc.scalar.activation(self.silu[:, s], self.g_ps[:], ACT.Silu, scale=1.0 / SPLIT).then_inc(self.silu_done, 1)
        act.wait_ge(self.h_done, b.times(nf, f + 1))
        need(act, self.down_mm, b.times(nf, f - 2))
        self.nc.scalar.copy(self.h_hi[:, f % 3], self.h_ps[:]).then_inc(self.hi_done, 1)

    def hidden(self, dve, b, n, f):
        if not b.live(n):
            return
        nf, s = self.nf, (b.slot(2) * self.nf + f) % 2
        dve.wait_ge(self.silu_done, b.times(nf, f + 1))
        dve.wait_ge(self.u_mm, b.times(nf, f + 1))
        need(dve, self.lo_done, b.times(nf, f))
        self.nc.vector.scalar_tensor_tensor(out=self.h_ps[:], in0=self.u_ps[:], scalar=1.0 / SPLIT, in1=self.silu[:, s],
                                            op0=ALU.mult, op1=ALU.mult).then_inc(self.h_done, 1)

    def rest(self, dve, b, n, f):
        if b.live(n):
            nf = self.nf
            dve.wait_ge(self.hi_done, b.times(nf, f + 1))
            need(dve, self.down_mm, b.times(nf, f - 2))
            self.nc.vector.tensor_tensor(self.h_lo[:, f % 3], self.h_ps[:], self.h_hi[:, f % 3],
                                         ALU.subtract).then_inc(self.lo_done, 1)


def make_down(nc, k, name, src, wd, nf):
    with Mem(nc, name) as m:
        nat = m.sb("nat", [P, 2, nf * P], F32)
        parts = m.sb("parts", [P, 2, 2, nf * P], F16)
        turned = [m.bank(f"turned{i}", F16)[:, 0:2 * D].rearrange("p (c n) -> p c n", c=2) for i in range(2)]
        loaded, hi_done, lo_done, turned_done, kept = (m.sem(x) for x in ("loaded", "hi", "lo", "turned_done", "kept"))
        halves = ((0, P), (1, REST))
        block = m.block()

        @block.sync
        def _(sp):
            for half, n in halves:
                sp.dma_start(nat[0:n, half], src[half * P:half * P + n, :]).then_inc(loaded, 16)

        @block.scalar
        def _(act):
            act.wait_ge(loaded, 32)
            for half, n in halves:
                nc.scalar.activation(parts[0:n, half, 0], nat[0:n, half], ACT.Copy, scale=SPLIT).then_inc(hi_done, 1)

        @block.vector
        def _(dve):
            for half, n in halves:
                dve.wait_ge(hi_done, half + 1)
                nc.vector.scalar_tensor_tensor(out=parts[0:n, half, 1], in0=nat[0:n, half], scalar=SPLIT,
                                               in1=parts[0:n, half, 0], op0=ALU.mult, op1=ALU.subtract).then_inc(lo_done, 1)
            for f in range(nf):
                dve.wait_ge(turned_done, f + 1)
                nc.vector.tensor_copy(wd[:, f], turned[f % 2]).then_inc(kept, 1)

        @block.tensor
        def _(pe):
            pe.wait_ge(lo_done, 2)
            for f in range(nf):
                need(pe, kept, f - 1)
                for part in range(2):
                    for half, n in halves:
                        last = pe.transpose(turned[f % 2][:, part, half * P:half * P + n],
                                            parts[0:n, half, part, f * P:(f + 1) * P], k["eye16"][0:n, 0:n])
                last.then_inc(turned_done, 1)


def block_rows(dram, b):
    part = dram[BLOCK * b.c:BLOCK * b.c + BLOCK, :] if isinstance(b.turn, int) else dram[bass.ds(b.times(BLOCK), BLOCK), :]
    return part.rearrange("(t p) d -> p t d", p=P)


def block_seqs(dram, b):
    q = BLOCK // SEQ
    part = dram[q * b.c:q * b.c + q] if isinstance(b.turn, int) else dram[bass.ds(b.times(q), q)]
    return part.rearrange("q p s d -> p q (s d)")


def block_of(tensor, b, width=1):
    at = b.times(width)
    return tensor[:, at:at + width] if isinstance(b.turn, int) else tensor[:, bass.ds(at, width)]


def gate_scores(nc, k, dims, gate, mv, chunks, scores, h1_dram, pack_dram):
    NT, E = dims["NT"], dims["E"]
    NK = NT // TILES
    with Mem(nc, "gates") as m:
        std = m.sb("std", [P, NT], F32)
        rstd = m.sb("rstd", [P, NT], F32)
        mean_rstd = m.sb("mean_rstd", [P, 2, TILES, 2], F32)
        h1 = m.sb("h1", [P, 2, TILES, D], F32)
        xn = m.sb("xn", [P, 2, TILES, D], F32)
        pack = m.sb("pack", [P, 2, TILES, PACK], F16)
        ring = m.sb("ring", [P, 2, 3, BLOCK], F16)
        c_ps = [m.bank(f"c_ps{i}", F16)[:].rearrange("p (c n) -> p c n", n=BLOCK) for i in range(2)]
        d_ps = [m.bank(f"d_ps{i}", F16)[:, 0:BLOCK] for i in range(2)]
        l_ps = [m.bank(f"l_ps{i}")[:, 0:TILES * E].rearrange("p (t e) -> p t e", e=E) for i in range(2)]
        (std_done, rstd_done, picked, xn_done, hi_done, lo_done, turned, first_kept, second_kept, logits_mm, logits_done,
         sig_done) = (m.sem(x) for x in (
             "std", "rstd", "picked", "xn", "hi", "lo", "turned", "first_kept", "second_kept", "logits_mm", "logits",
             "sig"))
        h1_in, pack_out, stored = m.sems("h1_in", 2), m.sems("pack_out", 2), m.sems("stored", 2)
        block = m.block()
        LAG, PERIOD = 3, 2

        @block.sync
        def _(sp):
            def step(i):
                t = i.back(-1)
                if t.live(NK):
                    need(sp, xn_done, t.times(1, -1))
                    sp.dma_start(h1[:, t.slot(2)].rearrange("p (q s) d -> p q (s d)", s=STEPS),
                                 block_seqs(h1_dram, t)).then_inc(h1_in[t.slot(2)], 16)
                t = i.back(1)
                if t.live(NK):
                    sp.wait_ge(lo_done, t.times(1, 1))
                    sp.dma_start(block_rows(pack_dram[:, 0:PACK // 2], t),
                                 pack[:, t.slot(2)].bitcast(U32)).then_inc(pack_out[t.slot(2)], 16)
                t = i.back(2)
                if t.live(NK):
                    sp.wait_ge(first_kept, t.times(1, 1))
                    sp.wait_ge(second_kept, t.times(1, 1))
                    sp.dma_start(block_of(chunks, t)[:, 0], ring[:, t.slot(2)]).then_inc(stored[t.slot(2)], 16)

            run_steps(sp, NK, 1, LAG, PERIOD, step)
            for a in range(2):
                sp.wait_ge(pack_out[a], 16 * ((NK - a + 1) // 2))
                sp.wait_ge(stored[a], 16 * ((NK - a + 1) // 2))

        @block.vector
        def _(dve):
            dve.wait_ge(std_done, 1)
            nc.vector.reciprocal(rstd[:], std[:]).then_inc(rstd_done, 1)
            dve.wait_ge(rstd_done, 1)

            def step(i):
                if i.live(NK):
                    a = i.slot(2)
                    need(dve, xn_done, i.times(1, -1))
                    nc.vector.tensor_copy(mean_rstd[:, a, :, 0], block_of(mv, i, TILES)[:, :, 0])
                    nc.vector.tensor_copy(mean_rstd[:, a, :, 1], block_of(rstd, i, TILES)).then_inc(picked, 1)
                    dve.wait_ge(picked, i.times(1, 1))
                    dve.wait_ge(h1_in[a], i.use(2, 16, 16))
                    need(dve, lo_done, i.times(1, -1))
                    for t in range(TILES):
                        last = nc.vector.tensor_scalar(xn[:, a, t, :], h1[:, a, t, :], mean_rstd[:, a, t, 0:1],
                                                       mean_rstd[:, a, t, 1:2], ALU.subtract, ALU.mult)
                    last.then_inc(xn_done, 1)
                b = i.back(3)
                if b.live(NK):
                    dve.wait_ge(logits_mm, b.times(1, 1))
                    nc.vector.tensor_scalar(block_of(scores, b, TILES), l_ps[b.slot(2)], 1.0 / SPLIT, None,
                                            ALU.mult).then_inc(logits_done, 1)
                b = i.back(2)
                if b.live(NK):
                    dve.wait_ge(turned, b.times(1, 1))
                    need(dve, logits_mm, b.times(1, -1))
                    need(dve, stored[b.slot(2)], b.use(2, 16))
                    nc.vector.tensor_copy(ring[:, b.slot(2), 2, :], d_ps[b.slot(2)]).then_inc(second_kept, 1)

            run_steps(dve, NK, 0, LAG, PERIOD, step)

        @block.scalar
        def _(act):
            nc.scalar.activation(std[:], mv[:, :, 1], ACT.Sqrt, bias=k["eps"][:]).then_inc(std_done, 1)

            def step(i):
                t = i.back(1)
                if t.live(NK):
                    a = t.slot(2)
                    act.wait_ge(xn_done, t.times(1, 1))
                    need(act, turned, t.times(1, -1))
                    need(act, pack_out[a], t.use(2, 16))
                    nc.scalar.copy(pack[:, a, :, 0:D], xn[:, a]).then_inc(hi_done, 1)
                b = i.back(2)
                if b.live(NK):
                    act.wait_ge(turned, b.times(1, 1))
                    need(act, logits_mm, b.times(1, -1))
                    need(act, stored[b.slot(2)], b.use(2, 16))
                    nc.scalar.copy(ring[:, b.slot(2), 0:2, :], c_ps[b.slot(2)]).then_inc(first_kept, 1)

            run_steps(act, NK, 0, LAG, PERIOD, step)
            act.wait_ge(logits_done, NK)
            nc.scalar.activation(scores[:], scores[:], ACT.Sigmoid).then_inc(sig_done, 1)

        @block.gpsimd
        def _(pool):
            def step(i):
                t = i.back(1)
                if t.live(NK):
                    a = t.slot(2)
                    pool.wait_ge(hi_done, t.times(1, 1))
                    nc.gpsimd.tensor_tensor(pack[:, a, :, D:2 * P], xn[:, a, :, P:D], pack[:, a, :, P:D], ALU.subtract)
                    nc.gpsimd.tensor_tensor(pack[:, a, :, 2 * P:PACK], xn[:, a, :, 0:P], pack[:, a, :, 0:P],
                                            ALU.subtract).then_inc(lo_done, 1)

            run_steps(pool, NK, 0, LAG, PERIOD, step)

        @block.tensor
        def _(pe):
            def step(i):
                b = i.back(2)
                if b.live(NK):
                    a = b.slot(2)
                    pe.wait_ge(lo_done, b.times(1, 1))
                    need(pe, first_kept, b.times(1, -1))
                    need(pe, second_kept, b.times(1, -1))
                    for t in range(TILES):
                        for c in range(3):
                            cols = slice(t * P, (t + 1) * P)
                            last = pe.transpose(c_ps[a][:, c, cols] if c < 2 else d_ps[a][:, cols],
                                                pack[:, a, t, c * P:(c + 1) * P], k["eye16"][:])
                    last.then_inc(turned, 1)
                b = i.back(3)
                if b.live(NK):
                    pe.wait_ge(first_kept, b.times(1, 1))
                    pe.wait_ge(second_kept, b.times(1, 1))
                    need(pe, logits_done, b.times(1, -1))
                    for t in range(TILES):
                        for c, (s, x) in enumerate(CHUNKS):
                            last = pe.matmul(l_ps[b.slot(2)][:, t, :], ring[:, b.slot(2), x, t * P:(t + 1) * P],
                                             gate[:, s, :], start=c == 0, stop=c == len(CHUNKS) - 1)
                    last.then_inc(logits_mm, 1)

            run_steps(pe, NK, 0, LAG, PERIOD, step)


BITS = 30


def shared_expert(nc, k, dims, w, chunks, scores, found, side, same, h1_dram, pack_dram, out_dram):
    NT, E, cap = dims["NT"], dims["E"], dims["cap"]
    NK = NT // TILES
    G = NT * E // P
    SUB = P // E
    nf = dims["FS"] // P
    inv = 1.0 / SPLIT
    PERIOD = 6
    assert NK >= BITS and nf == 3 and G % 4 == 0 and (NK - 1) // PERIOD * PERIOD <= BITS
    with Mem(nc, "shared") as m:
        out_done = m.sem("out")
        ff = FeedForward(nc, m, nf, out_done, turns=False)
        h1 = m.sb("h1", [P, 3, TILES, D], F32)
        out = m.sb("out", [P, 2, TILES, D], F32)
        mask = m.sb("mask", [P, G, P], F16)
        tiled_eye = m.sb("tiled_eye", [E, SUB, E], F32)
        count = m.sb("count", [P, 2], F32)
        bit, next_bit = (m.sb(x, [P, 1], F32) for x in ("bit", "next_bit"))
        delta, candidate, next_int = (m.sb(x, [P, 1], I32) for x in ("delta", "candidate", "next_int"))
        turn_ps = [m.bank(f"turn{i}") for i in range(2)]
        small = m.bank("small")
        (sided, side_done, same_mm, same_done, counted, halved, count_mm, delta_done, found_done, candidate_done,
         moved) = (m.sem(x) for x in (
             "sided", "side_done", "same_mm", "same_done", "counted", "halved", "count_mm", "delta_done", "found_done",
             "candidate_done", "moved"))
        h1_in, base_out, score_out = m.sems("h1_in", 3), m.sems("base_out", 2), m.sem("score_out")
        block = m.block()

        @block.sync
        def _(sp):
            def step(i):
                if i.live(NK):
                    need(sp, out_done, i.times(1, -2))
                    sp.dma_start(h1[:, i.slot(3)].rearrange("p (q s) d -> p q (s d)", s=STEPS),
                                 block_seqs(h1_dram, i)).then_inc(h1_in[i.slot(3)], 16)
                store_scores(i)
                t = i.back(1)
                if t.live(NK):
                    sp.wait_ge(out_done, t.times(1, 1))
                    sp.dma_start(block_rows(out_dram, t), out[:, t.slot(2)]).then_inc(base_out[t.slot(2)], 16)

            def store_scores(i):
                if i.live(NK):
                    sp.dma_start(block_rows(pack_dram[:, PACK // 2:PACK // 2 + E], i),
                                 block_of(scores, i, TILES).bitcast(U32)).then_inc(score_out, 16)

            run_steps(sp, NK, 0, 1, PERIOD, step)
            sp.wait_ge(score_out, 16 * NK)
            for a in range(2):
                sp.wait_ge(base_out[a], 16 * ((NK - a + 1) // 2))

        @block.vector
        def _(dve):
            nc.vector.memset(found[:], 0)
            nc.vector.memset(candidate[:], 1 << (BITS - 1)).then_inc(candidate_done, 1)
            nc.vector.memset(bit[:], 2.0 ** (BITS - 1)).then_inc(moved, 1)
            nc.vector.tensor_copy(tiled_eye[:], k["eye32"][0:E, None, 0:E].to_broadcast([E, SUB, E])).then_inc(same_done, 1)
            for g in range(0, G, 4):
                dve.wait_ge(sided, g // 4 + 1)
                nc.vector.tensor_copy(side[:, g:g + 4, :].rearrange("p g n -> p (g n)"), turn_ps[g // 4 % 2][:]).then_inc(side_done, 1)
            dve.wait_ge(same_mm, 1)
            nc.vector.tensor_copy(same[:], small[:, 0:P]).then_inc(same_done, 1)
            dve.wait_ge(side_done, G // 4)

            def compare(i, half):
                if i.live(BITS):
                    if half == 0:
                        dve.wait_ge(candidate_done, i.times(1, 1))
                        need(dve, count_mm, i.times(1, 0))
                    part = slice(half * G // 2, (half + 1) * G // 2)
                    nc.vector.tensor_scalar(mask[:, part], side[:, part], candidate[:].bitcast(F32), None, ALU.is_ge, ALU.add,
                                            accum_out=count[:, half:half + 1]).then_inc(counted, 1)

            def halve(i):
                if i.live(BITS):
                    dve.wait_ge(moved, i.times(1, 1))
                    nc.vector.tensor_scalar(next_bit[:], bit[:], 0.5, None, ALU.mult).then_inc(halved, 1)
                    dve.wait_ge(halved, i.times(2, 1))
                    nc.vector.tensor_copy(next_int[:], next_bit[:]).then_inc(halved, 1)

            def decide(i):
                if i.live(BITS):
                    dve.wait_ge(count_mm, i.times(1, 1))
                    nc.vector.tensor_scalar(delta[:], small[:, 0:1], cap - 0.5, bit[:], ALU.is_ge, ALU.mult).then_inc(delta_done, 1)
                    dve.wait_ge(delta_done, i.times(1, 1))
                    nc.vector.tensor_tensor(found[:], found[:], delta[:], ALU.bitwise_or).then_inc(found_done, 1)
                    nc.vector.tensor_copy(bit[:], next_bit[:]).then_inc(moved, 1)
                    dve.wait_ge(found_done, i.times(1, 1))
                    dve.wait_ge(halved, i.times(2, 2))
                    nc.vector.tensor_tensor(candidate[:], found[:], next_int[:], ALU.bitwise_or).then_inc(candidate_done, 1)

            def add(b):
                if b.live(NK):
                    dve.wait_ge(ff.down_mm, b.times(nf, nf))
                    need(dve, base_out[b.slot(2)], b.use(2, 16))
                    dve.wait_ge(h1_in[b.slot(3)], b.use(3, 16, 16))
                    for half in range(2):
                        two = slice(2 * half, 2 * half + 2)
                        last = nc.vector.scalar_tensor_tensor(
                            out=out[:, b.slot(2), two, :].rearrange("p t d -> p (t d)"), in0=ff.y_ps[:, half, 0:2 * D], scalar=inv,
                            in1=h1[:, b.slot(3), two, :].rearrange("p t d -> p (t d)"), op0=ALU.mult, op1=ALU.add)
                    last.then_inc(out_done, 1)

            def step(i):
                ff.hidden(dve, i, NK, 0)
                add(i.back(1))
                ff.rest(dve, i, NK, 0)
                decide(i.back(1))
                ff.hidden(dve, i, NK, 1)
                ff.rest(dve, i, NK, 1)
                compare(i, 0)
                ff.hidden(dve, i, NK, 2)
                ff.rest(dve, i, NK, 2)
                compare(i, 1)
                halve(i)

            run_steps(dve, NK, 0, 1, PERIOD, step)

        @block.scalar
        def _(act):
            def step(i):
                for f in range(nf):
                    ff.activate(act, i, NK, f)

            run_steps(act, NK, 0, 1, PERIOD, step)

        @block.tensor
        def _(pe):
            for g in range(0, G, 4):
                need(pe, side_done, g // 4 - 1)
                for j in range(4):
                    tiles = scores[:, (g + j) * SUB:(g + j + 1) * SUB, :].rearrange("p t e -> p (t e)")
                    last = pe.transpose(turn_ps[g // 4 % 2][:, j * P:(j + 1) * P], tiles, k["eye32"][:])
                last.then_inc(sided, 1)
            pe.wait_ge(same_done, 1)
            eyes = tiled_eye[:].rearrange("a s e -> a (s e)")
            pe.matmul(small[:, 0:P], eyes, eyes, start=True, stop=True).then_inc(same_mm, 1)
            pe.wait_ge(same_done, 2)

            def total(i):
                if i.live(BITS):
                    for half in range(2):
                        pe.wait_ge(counted, i.times(2, half + 1))
                        last = pe.matmul(small[:, 0:1], same[:], count[:, half:half + 1], start=half == 0, stop=half == 1)
                    last.then_inc(count_mm, 1)

            def step(i):
                b = i.back(1)
                for f in range(nf):
                    if i.live(NK):
                        ff.gate_up(pe, i, NK, f, w["sg"], w["su"], block_of(chunks, i)[:, 0])
                    ff.down(pe, i if f else b, NK, f - 1 if f else nf - 1, w["sd"])
                    if f == 0:
                        total(b)

            run_steps(pe, NK, 0, 1, PERIOD, step)


def choose_tokens(nc, k, dims, found, side, same, counts, before, upto):
    NT, E, cap = dims["NT"], dims["E"], dims["cap"]
    SUB = P // E
    G = NT // SUB
    PER = 8
    with Mem(nc, "choose") as m:
        above, equal = m.sb("above", [P, G, P], F16), m.sb("equal", [P, G, P], F16)
        above_t, equal_t = m.sb("above_t", [P, NT, E], F16), m.sb("equal_t", [P, NT, E], F16)
        chosen = m.sb("chosen", [P, NT, E], F16)
        spread = m.sb("spread", [P, NT, E], F16)
        less, up = m.sb("less", [P, P], F16), m.sb("up", [P, P], F16)
        ones, ones32 = m.sb("ones", [P, P], F16), m.sb("ones32", [P, P], F32)
        missing_rows = m.sb("missing_rows", [P, P], F32)
        missing_sb = m.sb("missing_sb", [P, E], F32)
        totals16 = m.sb("totals16", [P, E], F16)
        count, missing = m.sb("count", [P, 1], F32), m.sb("missing", [P, 1], F32)
        wide = [m.bank(f"wide{i}") for i in range(4)]
        small = m.bank("small")
        turn_ps = [m.bank(f"turn{i}") for i in range(2)]
        (cleared, triangles, counted, count_mm, masks, missing_done, rows_done, back, kept, tot_mm, tot_done,
         spread_done, rank_mm, ranked, chosen_a, chosen_b, count_in, counts_done, tots, before_mm, end,
         need_mm, need_done) = (m.sem(x) for x in (
            "cleared", "triangles", "counted", "count_mm", "masks", "missing_done", "rows_done", "back",
            "kept", "tot_mm", "tot_done", "spread_done", "rank_mm", "ranked", "chosen_a", "chosen_b",
            "count_in", "counts_done", "tots", "before_mm", "end", "need_mm", "need_done"))
        WN = 512 // E
        NW = -(-NT // WN)
        EW = 512 // P
        block = m.block()

        @block.gpsimd
        def _(pool):
            nc.gpsimd.memset(less[:], 1.0).then_inc(cleared, 1)
            nc.gpsimd.memset(up[:], 1.0).then_inc(cleared, 1)
            pool.wait_ge(cleared, 2)
            for tri, base in ((less, -1), (up, 0)):
                nc.gpsimd.affine_select(out=tri[:], in_=tri[:], compare_op=ALU.is_ge, fill=0.0, base=base,
                                        pattern=[[1, P]], channel_multiplier=-1).then_inc(triangles, 1)

        @block.vector
        def _(dve):
            nc.vector.memset(ones[:], 1.0)
            nc.vector.memset(ones32[:], 1.0)
            limit = found[:].bitcast(F32)
            nc.vector.tensor_scalar(above[:], side[:], limit, None, ALU.is_gt, ALU.add, accum_out=count[:]).then_inc(counted, 1)
            nc.vector.tensor_scalar(equal[:], side[:], limit, None, ALU.is_equal).then_inc(masks, 1)
            dve.wait_ge(count_mm, 1)
            nc.vector.tensor_scalar(missing[:], small[:, 0:1], -1.0, float(cap), ALU.mult, ALU.add).then_inc(missing_done, 1)
            dve.wait_ge(missing_done, 1)
            nc.vector.tensor_scalar(missing_rows[:], ones32[:], missing[:], None, ALU.mult).then_inc(rows_done, 1)
            dve.wait_ge(need_mm, 1)
            nc.vector.tensor_copy(missing_sb[:], small[:, 32:32 + E]).then_inc(need_done, 1)
            dve.wait_ge(tot_mm, 1)
            nc.vector.tensor_copy(totals16[0:NT, :], small[0:NT, 64:64 + E]).then_inc(tot_done, 1)
            dve.wait_ge(tot_done, 1)
            dve.wait_ge(triangles, 2)
            nc.vector.tensor_tensor(spread[0:NT], totals16[0:NT, None, :].to_broadcast([NT, NT, E]),
                                    less[0:NT, 0:NT, None].to_broadcast([NT, NT, E]), ALU.mult).then_inc(spread_done, 1)
            dve.wait_ge(rank_mm, 1)
            dve.wait_ge(need_done, 1)
            for w in range(NW):
                n = min(WN, NT - w * WN)
                nc.vector.tensor_tensor(chosen[:, w * WN:w * WN + n, :], wide[w][:, 0:n * E].rearrange("p (t e) -> p t e", e=E),
                                        missing_sb[:, None, :].to_broadcast([P, n, E]), ALU.is_lt).then_inc(ranked, 1)
            dve.wait_ge(ranked, NW)
            nc.vector.tensor_tensor(chosen[:], chosen[:], equal_t[:], ALU.mult).then_inc(chosen_a, 1)
            dve.wait_ge(chosen_a, 1)
            nc.vector.tensor_tensor(chosen[:], chosen[:], above_t[:], ALU.add).then_inc(chosen_b, 1)
            dve.wait_ge(count_in, 1)
            for w in range(E // EW):
                nc.vector.tensor_copy(counts[0:NT, w * EW:(w + 1) * EW, :],
                                      wide[w][0:NT, :].rearrange("p (e n) -> p e n", n=P)).then_inc(counts_done, 1)
            dve.wait_ge(counts_done, E // EW)
            nc.vector.tensor_copy(totals16[0:NT, :], counts[0:NT, :, P - 1]).then_inc(tots, 1)
            dve.wait_ge(before_mm, 1)
            nc.vector.tensor_copy(before[0:NT, :], small[0:NT, 96:96 + E]).then_inc(end, 1)
            dve.wait_ge(end, 1)
            nc.vector.tensor_tensor(upto[0:NT, :], before[0:NT, :], totals16[0:NT, :], ALU.add).then_inc(end, 1)

        @block.scalar
        def _(act):
            for n in range(2 * -(-G // PER)):
                which, g = n % 2, n // 2 * PER
                groups = min(PER, G - g)
                act.wait_ge(back, n + 1)
                nc.scalar.copy((above_t, equal_t)[which][:, g * SUB:(g + groups) * SUB, :].rearrange("p t e -> p (t e)"),
                               turn_ps[n % 2][:].bitcast(F16)[:, 0:groups * P]).then_inc(kept, 1)

        @block.tensor
        def _(pe):
            pe.wait_ge(counted, 1)
            pe.matmul(small[:, 0:1], same[:], count[:], start=True, stop=True).then_inc(count_mm, 1)
            pe.wait_ge(rows_done, 1)
            pe.matmul(small[:, 32:32 + E], missing_rows[:], k["eye32"][:, 0:E], start=True, stop=True).then_inc(need_mm, 1)
            pe.wait_ge(masks, 1)
            for n in range(2 * -(-G // PER)):
                which, g = n % 2, n // 2 * PER
                need(pe, kept, n - 1)
                for j in range(min(PER, G - g)):
                    last = pe.transpose(turn_ps[n % 2][:].bitcast(F16)[:, j * P:(j + 1) * P], (above, equal)[which][:, g + j, :],
                                        k["eye16"][:])
                last.then_inc(back, 1)
            pe.wait_ge(kept, 2 * -(-G // PER))
            pe.wait_ge(need_done, 1)
            for e in range(E):
                last = pe.matmul(small[0:NT, 64 + e:65 + e], equal_t[:, :, e], ones[:, 0:1], start=True, stop=True)
            last.then_inc(tot_mm, 1)
            pe.wait_ge(spread_done, 1)
            for w in range(NW):
                n = min(WN, NT - w * WN)
                tiles = slice(w * WN, w * WN + n)
                pe.matmul(wide[w][:, 0:n * E], less[:], equal_t[:, tiles, :].rearrange("p t e -> p (t e)"),
                          start=True, stop=False)
                last = pe.matmul(wide[w][:, 0:n * E], ones[0:NT, :], spread[0:NT, tiles, :].rearrange("p t e -> p (t e)"),
                                 start=False, stop=True)
            last.then_inc(rank_mm, 1)
            pe.wait_ge(chosen_b, 1)
            for e in range(E):
                last = pe.matmul(wide[e // EW][0:NT, e % EW * P:(e % EW + 1) * P], chosen[:, :, e], up[:], start=True, stop=True)
            last.then_inc(count_in, 1)
            pe.wait_ge(tots, 1)
            pe.matmul(small[0:NT, 96:96 + E], less[0:NT, 0:NT], totals16[0:NT, :], start=True, stop=True).then_inc(before_mm, 1)


def experts(nc, k, dims, counts, before, upto, wg_dram, wu_dram, wd_dram, pack_dram, out_dram):
    NT, E, cap = dims["NT"], dims["E"], dims["cap"]
    nf = dims["F"] // P
    per = cap // BLOCK
    n = E * per
    ZT = cap // P
    inv = 1.0 / SPLIT
    ROW = PACK // 2 + E
    assert per == 4 and nf == 6 and cap <= 2048 and NT <= P
    PERIOD = 2 * per
    LEAD = per - 1

    pieces = {q: [p for p in range(nf) if p * per // nf == q] for q in range(per)}
    jobs, order = {}, {}
    for q in range(per):
        if (q - LEAD) % per == per - 2:
            jobs[q] = {1: ("rows", 0), 3: ("rows", 1), 5: ("rows", 2), 7: ("rows", 3), 9: ("ids", 0),
                       10: ("first", pieces[q][0]), 11: ("second", pieces[q][0])}
            assert len(pieces[q]) == 1
        else:
            places = ((2, 4), (8, 10))
            jobs[q] = {place: (kind, p) for p, at in zip(pieces[q], places)
                       for place, kind in zip(at, ("first", "second"))}
        for place in sorted(jobs[q]):
            order[q, place] = len(order)
    SHARES = len(order)
    IDS_AT = order[(LEAD + per - 2) % per, 9]

    with Mem(nc, "experts") as m:
        y_done = m.sem("y_done")
        ff = FeedForward(nc, m, nf, y_done)
        wg, wu = m.sb("wg", [P, 2, 4, nf * P], F16), m.sb("wu", [P, 2, 4, nf * P], F16)
        wd = m.sb("wd", [P, 2, nf, 2, D], F16)
        nat = m.sb("nat", [P, 2, nf, D], F32)
        nat_d = m.sb("nat_d", [P, 2, nf * P], F32)
        parts = m.sb("parts", [P, 2, 2, 4 * P], F16)
        parts_d = m.sb("parts_d", [P, 2, 2, 2, P], F16)
        slots = m.sb("slots", [P, cap], F32)
        limits = m.sb("limits", [P, 2], F32)
        reach = m.sb("reach", [P, P], F16)
        past = m.sb("past", [P, cap], F16)
        own = m.sb("own", [P, cap], F16)
        earlier = m.sb("earlier", [P, cap], F16)
        hundred, one = m.sb("hundred", [P, 1], F16), m.sb("one", [P, 1], F16)
        ids = m.sb("ids", [P, 2, ZT], U32)
        rows = m.sb("rows", [P, 2, TILES, ROW], U32)
        score = m.sb("score", [P, 4, TILES], F32)
        y = m.sb("y", [P, 2, TILES, D], F32)
        shared = m.bank("shared")
        (w_hi, w_lo, w_twice, w_first, w_second, kept, set_up, nat_in, limits_done, reach_done, past_done,
         own_done, rows_mm, ids_mm, score_done, apart) = (m.sem(x) for x in (
             "w_hi", "w_lo", "w_twice", "w_first", "w_second", "kept", "set_up", "nat_in",
             "limits", "reach", "past", "own", "rows_mm", "ids_mm", "score", "apart"))
        got, added = m.sems("got", 2), m.sems("added", 2)
        halves = ((0, P), (1, REST))
        block = m.block()

        def expert(t):
            return t.use(per)

        def column(tensor, t):
            return tensor[:, t.c // per:t.c // per + 1] if isinstance(t.turn, int) else tensor[:, bass.ds(expert(t), 1)]

        def places(i, do):
            t = i.back(-LEAD)
            q = t.slot(per)

            def at(place):
                if t.live(n) and place in jobs[q]:
                    kind, what = jobs[q][place]
                    do(t, kind, what, t.use(per, SHARES, order[q, place]))
            return at

        def piece(t, p, plus=0):
            return t.use(per, nf, p + plus)

        @block.sync
        def _(sp):
            def load(t):
                if t.live(n) and t.slot(per) == 0:
                    need(sp, w_lo, t.use(per, nf, 0))
                    e = t.c // per if isinstance(t.turn, int) else expert(t)
                    for j, w in enumerate((wg_dram, wu_dram)):
                        sp.dma_start(nat[:, j], w[e].rearrange("(f p) d -> p f d", p=P)).then_inc(nat_in, 16)
                    for half, rows_n in halves:
                        sp.dma_start(nat_d[0:rows_n, half], wd_dram[e][half * P:half * P + rows_n, :]).then_inc(nat_in, 16)

            run_steps(sp, n, LEAD + 1, 0, PERIOD, lambda i: load(i.back(-LEAD - 1)))

        @block.gpsimd
        def _(pool):
            nc.gpsimd.iota(slots[:], pattern=[[1, cap]], base=0, channel_multiplier=0,
                           allow_small_or_imprecise_dtypes=True).then_inc(set_up, 1)

            def step(i):
                t = i.back(-1)
                if t.live(n):
                    a, q = t.slot(2), t.slot(per)
                    if q == 0:
                        need(pool, kept, t.use(per, SHARES, IDS_AT + 1), apart)
                    need(pool, ff.turned, t.times(1, -1))
                    need(pool, score_done, t.times(1, -1), apart)
                    for s in range(TILES):
                        z = q * TILES + s
                        nc.gpsimd.indirect_dma_start(
                            out=rows[:, a, s, :], out_offset=None, in_=pack_dram,
                            in_offset=bass.IndirectOffsetOnAxis(ap=ids[:, t.slot(PERIOD) // per, z:z + 1], axis=0)
                        ).then_inc(got[a], 16)
                t = i.back(-LEAD)
                if t.live(n):
                    for p in pieces[t.slot(per)]:
                        need(pool, w_lo, piece(t, p, 1), apart)
                        for c in (0, 2 * P):
                            last = nc.gpsimd.tensor_copy(parts[:, p % 2, :, c + D:c + 2 * P], parts[:, p % 2, :, c + P:c + D])
                        last.then_inc(w_twice, 1)
                t = i.back(2)
                if t.live(n):
                    a, q = t.slot(2), t.slot(per)
                    if q == 0:
                        for s in range(2):
                            need(pool, added[s], t.use(per, 16 * TILES * per // 2))
                    need(pool, y_done, t.times(1, 1), apart)
                    for s in range(TILES):
                        z = q * TILES + s
                        nc.gpsimd.indirect_dma_start(
                            out=out_dram, in_=y[:, a, s, :], in_offset=None, compute_op=ALU.add,
                            out_offset=bass.IndirectOffsetOnAxis(ap=ids[:, t.slot(PERIOD) // per, z:z + 1], axis=0)
                        ).then_inc(added[a], 16)

            run_steps(pool, n, LEAD, 2, PERIOD, step)
            for s in range(2):
                pool.wait_ge(added[s], 16 * TILES * n // 2)

        @block.scalar
        def _(act):
            def split(i, which):
                t = i.back(-LEAD)
                if not t.live(n) or which >= len(pieces[t.slot(per)]):
                    return
                p = pieces[t.slot(per)][which]
                if p == 0:
                    act.wait_ge(nat_in, t.use(per, 64, 64))
                need(act, w_second, piece(t, p, -1))
                nc.scalar.activation(parts[:, p % 2, :, 0:D], nat[:, :, p, :], ACT.Copy, scale=SPLIT)
                for half, rows_n in halves:
                    last = nc.scalar.activation(parts_d[0:rows_n, p % 2, half, 0, :], nat_d[0:rows_n, half, p * P:(p + 1) * P],
                                                ACT.Copy, scale=SPLIT)
                last.then_inc(w_hi, 1)

            def step(i):
                b = i.back(1)
                split(i, 0)
                ff.activate(act, b, n, 0)
                ff.activate(act, b, n, 1)
                split(i, 1)
                ff.activate(act, b, n, 2)
                ff.activate(act, b, n, 3)
                ff.keep_chunks(act, i, n)
                ff.activate(act, b, n, 4)
                ff.activate(act, b, n, 5)

            run_steps(act, n, LEAD, 2, PERIOD, step)

        @block.vector
        def _(dve):
            nc.vector.memset(hundred[:], float(P))
            nc.vector.memset(one[:], 1.0).then_inc(set_up, 1)
            dve.wait_ge(set_up, 2)

            def split(i, which):
                t = i.back(-LEAD)
                if not t.live(n) or which >= len(pieces[t.slot(per)]):
                    return
                p = pieces[t.slot(per)][which]
                dve.wait_ge(w_hi, piece(t, p, 1))
                nc.vector.scalar_tensor_tensor(out=parts[:, p % 2, :, 2 * P:2 * P + D], in0=nat[:, :, p, :], scalar=SPLIT,
                                               in1=parts[:, p % 2, :, 0:D], op0=ALU.mult, op1=ALU.subtract)
                for half, rows_n in halves:
                    last = nc.vector.scalar_tensor_tensor(
                        out=parts_d[0:rows_n, p % 2, half, 1, :], in0=nat_d[0:rows_n, half, p * P:(p + 1) * P], scalar=SPLIT,
                        in1=parts_d[0:rows_n, p % 2, half, 0, :], op0=ALU.mult, op1=ALU.subtract)
                last.then_inc(w_lo, 1)

            def prepare_ids(i, part):
                t = i.back(-LEAD)
                if not t.live(n) or t.slot(per) != 0:
                    return
                if part == 0:
                    nc.vector.tensor_copy(limits[0:NT, 0:1], column(before, t)[0:NT])
                    nc.vector.tensor_copy(limits[0:NT, 1:2], column(upto, t)[0:NT]).then_inc(limits_done, 1)
                    dve.wait_ge(limits_done, t.use(per, 1, 1))
                    need(dve, ids_mm, t.use(per, 1, 0))
                    mine = counts[0:NT, t.c // per, :] if isinstance(t.turn, int) else counts[0:NT, bass.ds(expert(t), 1), :]
                    nc.vector.tensor_scalar(reach[0:NT, :], mine, limits[0:NT, 0:1], None, ALU.add).then_inc(reach_done, 1)
                elif part <= 4:
                    cols = slice((part - 1) * 512, part * 512)
                    nc.vector.tensor_scalar(past[0:NT, cols], slots[0:NT, cols], limits[0:NT, 1:2], None,
                                            ALU.is_ge).then_inc(past_done, 1)
                    dve.wait_ge(past_done, t.use(per, 4, part))
                    nc.vector.scalar_tensor_tensor(out=own[0:NT, cols], in0=slots[0:NT, cols], scalar=limits[0:NT, 0:1],
                                                   in1=past[0:NT, cols], op0=ALU.is_ge, op1=ALU.subtract).then_inc(own_done, 1)

            def job(t, kind, what, share):
                parity = t.slot(PERIOD) // per
                if kind == "first":
                    dve.wait_ge(w_first, piece(t, what, 1))
                    if what == 0:
                        need(dve, ff.down_mm, t.use(per, nf * per, -nf * per))
                    cols = slice(what * P, (what + 1) * P)
                    turned = shared[:].bitcast(F16).rearrange("p (j c n) -> p j c n", j=2, c=4)
                    nc.vector.tensor_copy(wg[:, parity, :, cols], turned[:, 0])
                    nc.vector.tensor_copy(wu[:, parity, :, cols], turned[:, 1]).then_inc(kept, 1)
                if kind == "second":
                    dve.wait_ge(w_second, piece(t, what, 1))
                    nc.vector.tensor_copy(wd[:, parity, what], shared[:].bitcast(F16)[:, 0:2 * D].rearrange(
                        "p (c n) -> p c n", c=2)).then_inc(kept, 1)
                if kind == "rows":
                    dve.wait_ge(rows_mm, t.use(per, 4, what + 1))
                    cols = slice(what * 512, (what + 1) * 512)
                    nc.vector.tensor_tensor(earlier[:, cols], shared[:], slots[:, cols], ALU.is_le).then_inc(kept, 1)
                if kind == "ids":
                    dve.wait_ge(ids_mm, t.use(per, 1, 1))
                    for s in range(2):
                        need(dve, added[s], t.use(per, 16 * TILES * per // 2, -16 * TILES * per // 2))
                    nc.vector.tensor_copy(ids[:, parity, :], shared[:, 0:ZT]).then_inc(kept, 1)

            def keep_scores(t):
                if t.live(n):
                    need(dve, got[t.slot(2)], t.use(2, 16 * TILES, 16 * TILES), apart)
                    words = rows[:, t.slot(2)].bitcast(F32)
                    at = PACK // 2
                    mine = words[:, :, at + t.c // per] if isinstance(t.turn, int) else words[:, :, bass.ds(expert(t) + at, 1)]
                    nc.vector.tensor_copy(score[:, t.slot(4), :], mine).then_inc(score_done, 1)

            def scale(t):
                if t.live(n):
                    a = t.slot(2)
                    dve.wait_ge(ff.down_mm, t.times(nf, nf))
                    need(dve, added[a], t.use(2, 16 * TILES))
                    for s in range(TILES):
                        last = nc.vector.tensor_scalar(y[:, a, s, :], ff.y_tile(s), score[:, t.slot(4), s:s + 1], inv,
                                                       ALU.mult, ALU.mult)
                    last.then_inc(y_done, 1)

            def step(i):
                b, last = i.back(1), i.back(2)
                at = places(i, job)
                split(i, 0)
                for f in range(nf):
                    prepare_ids(i, f)
                    ff.hidden(dve, b, n, f)
                    if f == 0:
                        scale(last)
                        ff.rest(dve, b, n, f)
                    if f == 2:
                        split(i, 1)
                    if f == 3:
                        keep_scores(i)
                    at(2 * f)
                    if f:
                        ff.rest(dve, b, n, f)
                    at(2 * f + 1)

            run_steps(dve, n, LEAD, 2, PERIOD, step)

        @block.tensor
        def _(pe):
            pe.wait_ge(set_up, 2)

            def job(t, kind, what, share):
                need(pe, kept, share)
                if kind == "first":
                    pe.wait_ge(w_twice, piece(t, what, 1))
                    turned = shared[:].bitcast(F16).rearrange("p (j c n) -> p j c n", j=2, c=4)
                    for j in range(2):
                        for c in range(4):
                            last = pe.transpose(turned[:, j, c, :], parts[:, what % 2, j, c * P:(c + 1) * P], k["eye16"][:])
                    last.then_inc(w_first, 1)
                if kind == "second":
                    turned = shared[:].bitcast(F16)[:, 0:2 * D].rearrange("p (c n) -> p c n", c=2)
                    for part in range(2):
                        for half, rows_n in halves:
                            last = pe.transpose(turned[:, part, half * P:half * P + rows_n],
                                                parts_d[0:rows_n, what % 2, half, part, :], k["eye16"][0:rows_n, 0:rows_n])
                    last.then_inc(w_second, 1)
                if kind == "rows":
                    if what == 0:
                        pe.wait_ge(reach_done, t.use(per, 1, 1))
                    pe.wait_ge(own_done, t.use(per, 4, what + 1))
                    pe.matmul(shared[:], reach[0:NT, :], own[0:NT, what * 512:(what + 1) * 512],
                              start=True, stop=True).then_inc(rows_mm, 1)
                if kind == "ids":
                    for z in range(ZT):
                        cols = slice(z * P, (z + 1) * P)
                        pe.matmul(shared[:, z:z + 1], past[0:NT, cols], hundred[0:NT, :], start=True, stop=False)
                        last = pe.matmul(shared[:, z:z + 1], earlier[:, cols], one[:], start=False, stop=True)
                    last.then_inc(ids_mm, 1)

            def step(i):
                b, last = i.back(1), i.back(2)
                parity = b.slot(PERIOD) // per
                at = places(i, job)
                if b.live(n) and b.slot(per) == 0:
                    pe.wait_ge(kept, b.use(per, SHARES, SHARES))
                if b.live(n):
                    pe.wait_ge(ff.chunks_done, b.times(1, 1))
                for f in range(nf):
                    ff.gate_up(pe, b, n, f, wg[:, parity], wu[:, parity], ff.chunks[:, b.slot(2)])
                    at(2 * f)
                    if f == 0:
                        ff.down(pe, last, n, nf - 1, wd[:, last.slot(PERIOD) // per])
                    else:
                        ff.down(pe, b, n, f - 1, wd[:, parity])
                    if f == 3:
                        if i.live(n):
                            pe.wait_ge(got[i.slot(2)], i.use(2, 16 * TILES, 16 * TILES))
                        ff.turn(pe, i, n, lambda t, s: rows[:, t.slot(2), s, 0:PACK // 2].bitcast(F16), k["eye16"])
                    at(2 * f + 1)

            run_steps(pe, n, LEAD, 2, PERIOD, step)


def language_model_block(nc, x, emb, ws, wqkv, w_out, b_out, gate, wg, wu, wd, ws_g, ws_u, ws_d, out):
    NT = x.shape[0]
    T = NT * P
    NB = T // SEQ
    E, F = wg.shape[0], wg.shape[1]
    FS = ws_g.shape[0]
    dims = dict(NT=NT, NB=NB, E=E, F=F, FS=FS, cap=T * 2 // E, group=GROUP)
    stack_dram = nc.dram_tensor("stack", [NB, 2 * HD + 2, HEADS * SEQ], F16).ap()
    v_dram = nc.dram_tensor("values", [NB, P, STEPS, VROW], F32).ap()
    h_dram = nc.dram_tensor("h", [NB, P, STEPS, D], F32).ap()
    h1_dram = nc.dram_tensor("h1", [NB, P, STEPS, D], F32).ap()
    pack_dram = nc.dram_tensor("packs", [T, PACK // 2 + E], U32).ap()
    with Mem(nc, "top") as top:
        k = make_constants(nc, top, ws, x, dims)
        mv = top.sb("mv", [P, NT, 2], F32)
        with Mem(nc, "kept") as kept:
            out_stack = kept.sb("w_out", [P, 4, D], F16)
            w = dict(gate=kept.sb("gate", [P, 4, E], F16), sg=kept.sb("sg", [P, 4, FS], F16),
                     su=kept.sb("su", [P, 4, FS], F16), sd=kept.sb("sd", [P, FS // P, 2, D], F16))
            with Mem(nc, "first") as m:
                wqkv_stack = m.sb("wqkv", [P, 4, 2 * D], F16)
                make_stacks(nc, k, "stacks", query_jobs(wqkv, wqkv_stack[:, :, 0:D])
                            + row_jobs(wqkv[D:2 * D, :], D, wqkv_stack[:, :, D:2 * D]) + row_jobs(w_out, D, out_stack)
                            + row_jobs(gate, E, w["gate"]) + row_jobs(ws_g, FS, w["sg"]) + row_jobs(ws_u, FS, w["su"]))
                make_down(nc, k, "down_weights", ws_d, w["sd"], FS // P)
                embed_and_project(nc, k, dims, emb, wqkv_stack, stack_dram, v_dram, h_dram)
            attention(nc, k, dims, out_stack, b_out, mv, stack_dram, v_dram, h_dram, h1_dram)
            counts = kept.sb("counts", [P, E, P], F16)
            before, upto = kept.sb("before", [P, E], F32), kept.sb("upto", [P, E], F32)
            found = kept.sb("found", [P, 1], I32)
            side, same = kept.sb("side", [P, NT * E // P, P], F32), kept.sb("same", [P, P], F32)
            with Mem(nc, "network") as n:
                scores = n.sb("scores", [P, NT, E], F32)
                chunks = n.sb("chunks", [P, NT // TILES, 3, BLOCK], F16)
                gate_scores(nc, k, dims, w["gate"], mv, chunks, scores, h1_dram, pack_dram)
                shared_expert(nc, k, dims, w, chunks, scores, found, side, same, h1_dram, pack_dram, out)
            choose_tokens(nc, k, dims, found, side, same, counts, before, upto)
            experts(nc, k, dims, counts, before, upto, wg, wu, wd, pack_dram, out)


def kernel(**inputs):
    import numpy as np
    import concourse.bacc as bacc
    from concourse import mybir
    from concourse.bass_utils import run_bass_kernel_spmd

    shapes = {"x": (-1, 128), "L0_tok_weight_scale": (1, 1), "L0_attn_b_out": (1, -1)}
    names = ["x", "L0_tok_weight", "L0_tok_weight_scale", "L0_attn_W_qkv", "L0_attn_W_out", "L0_attn_b_out",
             "L0_ffn_gate_weight", "L0_ffn_Wg", "L0_ffn_Wu", "L0_ffn_Wd", "L0_ffn_Ws_g", "L0_ffn_Ws_u", "L0_ffn_Ws_d"]
    nc = bacc.Bacc("TRN2", target_bir_lowering=False, num_devices=1)
    arrays, args = {}, []
    for name in names:
        a = np.ascontiguousarray(inputs[name])
        if name in shapes:
            a = a.reshape(shapes[name])
        arrays[f"in_{name}"] = a
        args.append(nc.dram_tensor(f"in_{name}", a.shape, mybir.dt.from_np(a.dtype), kind="ExternalInput").ap())
    tokens, d = inputs["x"].shape, inputs["L0_tok_weight"].shape[1]
    out = nc.dram_tensor("out", (tokens[0] * tokens[1], d), mybir.dt.float32, kind="ExternalOutput").ap()
    language_model_block(nc, *args, out)
    r = run_bass_kernel_spmd(nc, [arrays], core_ids=[0])
    return r.results[0]["out"].reshape(tokens[0], tokens[1], d)
```
